# Optimizing a Trainium2 kernel written in Bass

```python
import numpy as np
import jax
import jax.numpy as jnp

def _softmax(x, axis=-1):
    return jax.nn.softmax(x, axis=axis)

def _gelu(x):
    return jax.nn.gelu(x, approximate=True)

def _silu(x):
    return jax.nn.silu(x)

def _sigmoid(x):
    return jax.nn.sigmoid(x)

def _layernorm(x, axis=-1, eps=1e-05):
    m = jnp.mean(x, axis=axis, keepdims=True)
    v = jnp.var(x, axis=axis, keepdims=True)
    return (x - m) / jnp.sqrt(v + eps)

def _scatter_add(tgt, idx, src, axis=0):
    return tgt.at[idx].add(src)

def _segment_sum(src, seg, n):
    return jax.ops.segment_sum(src, seg, n)
kernel_name = 'mk_seq_postln_d1_jaxref_r8_ef050e'

def setup_inputs(seed: int=0):
    np.random.seed(seed)
    _w = jnp.asarray

    def _L0_attn_setup():
        import jax, jax.numpy as jnp
        import numpy as np
        import math
        B, S, D = (4, 256, 256)
        QK = D // 8
        EXP = D * 2
        RESIDUAL_DEPTH = 144
        NUM_BLOCKS = 24
        key = jax.random.key(seed)
        k_x, k_e, k_p = jax.random.split(key, 3)
        x = jax.random.normal(k_x, (B, S, D), jnp.float32)
        expand_scale = 0.5 / math.sqrt(RESIDUAL_DEPTH) / 2.0
        project_scale = 1.0 / math.sqrt(RESIDUAL_DEPTH) / 2.0 / NUM_BLOCKS
        expand = expand_scale * jax.random.normal(k_e, (2 * QK + 2 * EXP, D), jnp.float32)
        project = project_scale * jax.random.normal(k_p, (D, EXP), jnp.float32)
        return {'x': x, 'ln_gamma': jnp.ones((D,), jnp.float32), 'ln_beta': jnp.zeros((D,), jnp.float32), 'expand': expand, 'project': project, 'pos_mult': jnp.float32(1.0)}
    _L0_attn_in = _L0_attn_setup()

    def _L0_ffn_setup():
        import jax, jax.numpy as jnp
        import numpy as np
        B, S, D = (2, 256, 256)
        I = 128
        E = 32
        K = 4
        NS = 1
        ALPHA = 7.0

        def _clamped_swiglu(x, wg, wu, wd):
            g = jnp.clip(x @ wg.T, -ALPHA, ALPHA)
            u = jnp.clip(x @ wu.T, -ALPHA, ALPHA)
            return jax.nn.silu(g) * u @ wd.T
        key = jax.random.key(seed)
        ks = jax.random.split(key, 9)
        s = 0.02
        return {'hidden': jax.random.normal(ks[0], (B, S, D), jnp.float32), 'router_w': jax.random.normal(ks[1], (E, D), jnp.float32) * s, 'expert_bias': jax.random.normal(ks[2], (E,), jnp.float32) * s, 'gate_w': jax.random.normal(ks[3], (E, I, D), jnp.float32) * s, 'up_w': jax.random.normal(ks[4], (E, I, D), jnp.float32) * s, 'down_w': jax.random.normal(ks[5], (E, D, I), jnp.float32) * s, 'shared_gate_w': jax.random.normal(ks[6], (NS * I, D), jnp.float32) * s, 'shared_up_w': jax.random.normal(ks[7], (NS * I, D), jnp.float32) * s, 'shared_down_w': jax.random.normal(ks[8], (D, NS * I), jnp.float32) * s}
    _L0_ffn_in = _L0_ffn_setup()
    _d = {'L0_attn_x': _L0_attn_in['x'], 'L0_attn_ln_gamma': _L0_attn_in['ln_gamma'], 'L0_attn_ln_beta': _L0_attn_in['ln_beta'], 'L0_attn_expand': _L0_attn_in['expand'], 'L0_attn_project': _L0_attn_in['project'], 'L0_attn_pos_mult': _L0_attn_in['pos_mult'], 'L0_ffn_router_w': _L0_ffn_in['router_w'], 'L0_ffn_expert_bias': _L0_ffn_in['expert_bias'], 'L0_ffn_gate_w': _L0_ffn_in['gate_w'], 'L0_ffn_up_w': _L0_ffn_in['up_w'], 'L0_ffn_down_w': _L0_ffn_in['down_w'], 'L0_ffn_shared_gate_w': _L0_ffn_in['shared_gate_w'], 'L0_ffn_shared_up_w': _L0_ffn_in['shared_up_w'], 'L0_ffn_shared_down_w': _L0_ffn_in['shared_down_w']}
    _x0 = _d['L0_attn_x']
    _d['L0_attn_x'] = jax.random.normal(jax.random.fold_in(jax.random.key(seed), 1), (2, 512, 256), dtype=_x0.dtype)
    del _x0
    return _d

def reference(L0_attn_x, L0_attn_ln_gamma, L0_attn_ln_beta, L0_attn_expand, L0_attn_project, L0_attn_pos_mult, L0_ffn_router_w, L0_ffn_expert_bias, L0_ffn_gate_w, L0_ffn_up_w, L0_ffn_down_w, L0_ffn_shared_gate_w, L0_ffn_shared_up_w, L0_ffn_shared_down_w):

    def _L0_attn_ref(x, ln_gamma, ln_beta, expand, project, pos_mult):
        import jax, jax.numpy as jnp
        import numpy as np
        import math
        B, S, D = (4, 256, 256)
        QK = D // 8
        EXP = D * 2
        RESIDUAL_DEPTH = 144
        NUM_BLOCKS = 24
        Bx, Sx, Dx = x.shape
        qk_dim = Dx // 8
        expand_dim = Dx * 2
        v_dim = Dx
        idx = jnp.arange(Sx)
        rel = (idx[None, :] - idx[:, None]).astype(x.dtype)
        causal = idx[None, :] <= idx[:, None]
        attn_mask = jnp.where(causal, jax.nn.softplus(pos_mult) * rel, -jnp.inf)
        mu = x.mean(-1, keepdims=True)
        var = x.var(-1, keepdims=True)
        h = (x - mu) * jax.lax.rsqrt(var + 1e-05) * ln_gamma + ln_beta
        fused = jnp.einsum('bsd,ed->bse', h, expand)
        query = fused[..., :qk_dim]
        key_ = fused[..., qk_dim:2 * qk_dim]
        linear = fused[..., 2 * qk_dim:2 * qk_dim + expand_dim]
        pre_gelu = fused[..., 2 * qk_dim + expand_dim:]
        geglu = linear * jax.nn.gelu(pre_gelu, approximate=False)
        geglu_local = geglu[..., :expand_dim - v_dim]
        value = geglu[..., expand_dim - v_dim:]
        scale = 1.0 / math.sqrt(qk_dim)
        scores = jnp.einsum('bqd,bkd->bqk', query, key_) * scale + attn_mask
        attn = jnp.einsum('bqk,bkd->bqd', jax.nn.softmax(scores, axis=-1), value)
        out = jnp.einsum('bse,de->bsd', jnp.concatenate([geglu_local, attn], axis=-1), project)
        return x + out

    def _L0_ffn_ref(hidden, router_w, expert_bias, gate_w, up_w, down_w, shared_gate_w, shared_up_w, shared_down_w):
        import jax, jax.numpy as jnp
        import numpy as np
        B, S, D = (2, 256, 256)
        I = 128
        E = 32
        K = 4
        NS = 1
        ALPHA = 7.0

        def _clamped_swiglu(x, wg, wu, wd):
            g = jnp.clip(x @ wg.T, -ALPHA, ALPHA)
            u = jnp.clip(x @ wu.T, -ALPHA, ALPHA)
            return jax.nn.silu(g) * u @ wd.T
        Bb, Ss, Dd = hidden.shape
        flat = hidden.reshape(-1, Dd)
        T = flat.shape[0]
        logits = flat @ router_w.T
        scores = jnp.sqrt(jax.nn.softplus(logits))
        _, idx = jax.lax.top_k(scores + expert_bias, K)
        topv = jnp.take_along_axis(scores, idx, axis=1)
        topv = topv / (topv.sum(axis=-1, keepdims=True) + 1e-20)
        probs = jnp.zeros((T, E), flat.dtype).at[jnp.arange(T)[:, None], idx].set(topv)

        def body(acc, xs):
            wg, wu, wd, p = xs
            return (acc + p[:, None] * _clamped_swiglu(flat, wg, wu, wd), None)
        out, _ = jax.lax.scan(body, jnp.zeros_like(flat), (gate_w, up_w, down_w, probs.T))
        out = out + _clamped_swiglu(flat, shared_gate_w, shared_up_w, shared_down_w)
        return out.reshape(Bb, Ss, Dd)
    x = L0_attn_x
    x = _layernorm(x + _L0_attn_ref(x, L0_attn_ln_gamma, L0_attn_ln_beta, L0_attn_expand, L0_attn_project, L0_attn_pos_mult), axis=-1)
    x = _layernorm(x + _L0_ffn_ref(x, L0_ffn_router_w, L0_ffn_expert_bias, L0_ffn_gate_w, L0_ffn_up_w, L0_ffn_down_w, L0_ffn_shared_gate_w, L0_ffn_shared_up_w, L0_ffn_shared_down_w), axis=-1)
    return x

_drawn_inputs = setup_inputs


def setup_inputs(seed=0):
    import zlib

    import numpy as np

    out = dict(_drawn_inputs(seed))
    spreads = {'L0_attn_ln_gamma': (1.0, 0.6), 'L0_attn_ln_beta': (0.0, 0.8)}
    factors = {'L0_attn_expand': 8.0,
     'L0_attn_project': 8.0,
     'L0_ffn_router_w': 8.0,
     'L0_ffn_expert_bias': 8.0,
     'L0_ffn_gate_w': 8.0,
     'L0_ffn_up_w': 8.0,
     'L0_ffn_down_w': 8.0,
     'L0_ffn_shared_gate_w': 4.853,
     'L0_ffn_shared_up_w': 4.812,
     'L0_ffn_shared_down_w': 4.815}
    for name, (base, spread) in spreads.items():
        noise = np.random.default_rng([zlib.crc32(name.encode()), seed]).standard_normal(out[name].shape)
        drawn = base * np.exp(spread * noise) if base else spread * noise
        out[name] = jnp.asarray(drawn.astype(out[name].dtype))
    for name, factor in factors.items():
        out[name] = (out[name] * factor).astype(out[name].dtype)
    return out
```

```python
from contextlib import ExitStack

import concourse.bass as bass
from concourse import mybir

F32 = mybir.dt.float32
F16 = mybir.dt.float16
I32 = mybir.dt.int32
U32 = mybir.dt.uint32
ALU = mybir.AluOpType
ACT = mybir.ActivationFunctionType
AX = mybir.AxisListType.X

P = 128
B, S, D = 2, 512, 256
T = B * S // P
TB = S // P
DC = D // P
QK = D // 8
LOC = D
E, I, K = 32, 128, 4
EW = E + 1
SLOTS = 64
NEG = -1.0e30
EPS = 1e-5
ALPHA = 7.0
LN2 = 0.6931471805599453
SQ_UP = 50

C_ID, C_LT, C_ONE, C_IOTA = 0, P, 2 * P, 3 * P
C_REL, C_MASK = 4 * P, 4 * P + S
C_TOK = C_MASK + S
C_PID = C_TOK + T
C_TRI = C_PID + 1
NCONST = C_TRI + 2 * E

X_Q, X_K = 0, QK
X_LIN, X_PRE, X_VAL = 2 * QK, 2 * QK + LOC, 2 * QK + 2 * LOC
NEXP = 2 * QK + 4 * D


def attn_moe_program(nc, x, consts, small, rbias, expand, project, router, gate_up, down, out):
    x1_dram = nc.dram_tensor("x1_rows", [B * S, D], F32)
    y_dram = nc.dram_tensor("slot_rows", [SLOTS * P, D], F32)

    with ExitStack() as ctx:
        def sb(name, shape, dt=F32):
            return ctx.enter_context(nc.sbuf_tensor(name, shape, dt))

        def sem(name):
            return ctx.enter_context(nc.semaphore(name))

        bank = [ctx.enter_context(nc.psum_tensor(f"bank{n}", [P, 512], F32)) for n in range(8)]

        w_gu = sb("w_gu", [P, EW, DC, 2 * I])
        w_dn = sb("w_dn", [P, EW, D])
        cst = sb("cst", [P, NCONST])
        sml = sb("sml", [P, 2 * DC + 1])
        bias_e = sb("bias_e", [P, E])
        ex_w = sb("ex_w", [P, DC, NEXP])
        pj_w = sb("pj_w", [P, 2 * DC, D])
        rt_w = sb("rt_w", [P, DC, E])
        x_sb = sb("x_sb", [P, T, D])
        z_sb = sb("z_sb", [P, T, D])
        x1 = z_sb
        hT = sb("hT", [P, DC, B * S])
        x1T = hT
        qT = sb("qT", [QK, B * S])
        kT = sb("kT", [QK, B * S])
        locT = sb("locT", [P, DC, B * S])
        val = sb("val", [P, T, D])
        gl = sb("gl", [P, 2, S])
        gv = sb("gv", [P, 2, D])
        bmat = sb("bmat", [P, S])
        s_sb = sb("s_sb", [P, 2, S])
        p_sb = sb("p_sb", [P, 2, S])
        pT = sb("pT", [P, S])
        aT = sb("aT", [P, 2, D])
        y1 = sb("y1", [P, 2, D])
        bst = sb("bst", [P, T, 6])
        mv = sb("mv", [P, T, 2])
        rs = sb("rs", [P, T])
        nt = sb("nt", [P, T, 2])
        mxs = sb("mxs", [P, T, 4])
        pb = sb("pb", [P, 8])
        sc16 = sb("sc16", [P, 4 * P], F16)
        lg = sb("lg", [P, T, E])
        ra = sb("ra", [P, T, E])
        re_ = sb("re_", [P, T, E])
        rb = sb("rb", [P, T, E])
        rc = sb("rc", [P, T, E])
        score = sb("score", [P, T, E])
        sel = sb("sel", [P, T, E])
        top = sb("top", [P, T, 8])
        topi = sb("topi", [P, T, 8], U32)
        topf = sb("topf", [P, T, K])
        oh = sb("oh", [P, T, K, E], F16)
        prod = sb("prod", [P, T, K, E])
        pk = sb("pk", [P, T, K])
        psum_k = sb("psum_k", [P, T, 2])
        ntile_i = sb("ntile_i", [P, E], I32)
        ntile_j = sb("ntile_j", [P, E], I32)
        ntile = sb("ntile", [P, E])
        ntd = sb("ntd", [E, E])
        ntcol = sb("ntcol", [E, 1])
        base = sb("base", [P, E])
        ends = sb("ends", [P, E])
        posb = sb("posb", [P, T, E])
        slot_f = sb("slot_f", [P, T * K])
        slot_i = sb("slot_i", [P, T * K], I32)
        slot_t = sb("slot_t", [P, 2, T * K], I32)
        slot_r = sb("slot_r", [P, 2, T * K])
        te_col = sb("te_col", [P, 1])
        te_row = sb("te_row", [1, SLOTS], I32)
        token = sb("token", [P, SLOTS], I32)
        ohr = ex_w[:, :, :].rearrange("p c n -> p (c n)")[:, 0:T * K * P // 2].bitcast(F16)
        idt = gl[:, :, :].rearrange("p a n -> p (a n)").bitcast(F16).rearrange("p (n s) -> p n s", s=SLOTS)
        xg, y_sb = val[:, 0:4, :], val[:, 4:8, :]
        work = x_sb[:, :, :].rearrange("p t d -> p (t d)")

        def pair(at, width):
            return work[:, at:at + 2 * width].rearrange("p (a n) -> p a n", a=2)

        xT, gu = pair(0, D), pair(2 * D, 2 * I)
        sg, hh, hTs = pair(4 * D, I), pair(4 * D + 2 * I, I), pair(4 * D + 4 * I, P)
        shared = locT[:, :, :].rearrange("p c (t d) -> p (c t) d", d=D)
        yg = w_gu[:, 0:16, :, :].rearrange("p e c n -> p (e c n)").rearrange("p (j d) -> p j d", d=D)
        acc = s_sb[:, :, 0:D]
        fin = p_sb[:, :, 0:D]

        ident = cst[:, C_ID:C_ID + P]
        before16 = sc16[:, P:2 * P]
        ones16 = sc16[:, 2 * P:3 * P]
        iota16 = sc16[:, 3 * P:4 * P]

        ld_x = [sem(f"ld_x{b}") for b in range(B)]
        ld_c = sem("ld_c")
        ld_s = sem("ld_s")
        ld_ex = sem("ld_ex")
        ld_pj = sem("ld_pj")
        ld_sh = sem("ld_sh")
        ld_w = sem("ld_w")
        vec = sem("vec")
        act_ = sem("act_")
        consts_ready = sem("consts_ready")
        var_ready = sem("var_ready")
        rstd_ready = sem("rstd_ready")
        z_ready = sem("z_ready")
        zt_done = sem("zt_done")
        h_ready = sem("h_ready")
        ex_done = sem("ex_done")
        qk_ready = sem("qk_ready")
        gelu_ready = sem("gelu_ready")
        geglu_ready = sem("geglu_ready")
        pos_ready = sem("pos_ready")
        sc_done = sem("sc_done")
        smax_ready = sem("smax_ready")
        exp_ready = sem("exp_ready")
        p_ready = sem("p_ready")
        pt_done = sem("pt_done")
        pt_ready = sem("pt_ready")
        av_done = sem("av_done")
        at_ready = sem("at_ready")
        pj_done = sem("pj_done")
        y1_ready = sem("y1_ready")
        rstd2_ready = sem("rstd2_ready")
        x1_ready = sem("x1_ready")
        x1t_done = sem("x1t_done")
        x1t_ready = sem("x1t_ready")
        lg_done = sem("lg_done")
        x1_stored = sem("x1_stored")
        r_dve = sem("r_dve")
        r_act = sem("r_act")
        oh_ready = sem("oh_ready")
        pos_done = sem("pos_done")
        ntcol_ready = sem("ntcol_ready")
        start_done = sem("start_done")
        te_ready = sem("te_ready")
        ter_done = sem("ter_done")
        te_loaded = sem("te_loaded")
        ohr_ready = sem("ohr_ready")
        list_done = sem("list_done")
        token_ready = sem("token_ready")
        slots_ready = sem("slots_ready")
        gath = [sem(f"gath{n}") for n in range(4)]
        xt_done = sem("xt_done")
        xt_ready = sem("xt_ready")
        gu_done = sem("gu_done")
        clipped = sem("clipped")
        silu_ready = sem("silu_ready")
        hh_ready = sem("hh_ready")
        ht_done = sem("ht_done")
        ht_ready = sem("ht_ready")
        dn_done = sem("dn_done")
        y_ready = sem("y_ready")
        y_stored = [sem(f"y_stored{n}") for n in range(4)]
        yg_in = [sem(f"yg_in{t}") for t in range(T)]
        var3_ready = sem("var3_ready")
        rstd3_ready = sem("rstd3_ready")
        fin_ready = sem("fin_ready")
        out_stored = [sem(f"out_stored{n}") for n in range(2)]

        block = ctx.enter_context(nc.Block())

        JOBS = 6 + TB

        def released(n):
            b, j = divmod(n, JOBS)
            if j < 2:
                return qk_ready, 2 * b + j + 1
            if j in (2, 4):
                return gelu_ready, 6 * b + j // 2
            return geglu_ready, 6 * b + (j // 2 if j < 6 else j - 3)

        x_rows = x.rearrange("b (t p) d -> p (b t) d", p=P)
        out_rows = out.rearrange("b (t p) d -> p (b t) d", p=P)
        x1_rows = x1_dram.ap().rearrange("(t p) d -> p t d", p=P)
        y_rows = y_dram.ap()
        ST = T + SLOTS

        LAG_PT, LAG_AV, LAG_PJ, LAG_FIN, LAG_XT = 1, 2, 3, 4, 5

        @block.sync
        def _(sp):
            sp.dma_start(x_sb[:, 0:TB, :], x_rows[:, 0:TB, :]).then_inc(ld_x[0], 16)
            sp.dma_start(cst[:, :], consts).then_inc(ld_c, 16)
            sp.dma_start(sml[:, :], small).then_inc(ld_s, 16)
            sp.dma_start(bias_e[:, :], rbias.to_broadcast([P, E])).then_inc(ld_s, 16)
            sp.dma_start(x_sb[:, TB:T, :], x_rows[:, TB:T, :]).then_inc(ld_x[1], 16)
            sp.dma_start(ex_w[:, :, :], expand).then_inc(ld_ex, 16)
            sp.dma_start(pj_w[:, :, :], project).then_inc(ld_pj, 16)
            sp.dma_start(rt_w[:, :, :], router).then_inc(ld_pj, 16)
            sp.dma_start(w_gu[:, E:EW, :, :], gate_up[:, E:EW, :, :]).then_inc(ld_sh, 16)
            sp.dma_start(w_dn[:, E:EW, :], down[:, E:EW, :]).then_inc(ld_sh, 16)
            for c in range(0, E, 4):
                sp.dma_start(w_gu[:, c:c + 4, :, :], gate_up[:, c:c + 4, :, :]).then_inc(ld_w, 16)
                sp.dma_start(w_dn[:, c:c + 4, :], down[:, c:c + 4, :]).then_inc(ld_w, 16)
            for t in range(T):
                sp.wait_ge(x1_ready, t + 1)
                sp.dma_start(x1_rows[:, t, :], x1[:, t, :]).then_inc(x1_stored, 16)

            with sp.Fori(0, SLOTS // 4) as n:
                for j in range(4):
                    sp.wait_ge(y_ready, 4 * n + (T + j + 1))
                    sp.dma_start(y_rows[bass.ds(n * (4 * P) + j * P, P), :], y_sb[:, j, :]).then_inc(y_stored[j], 16)
            for t in range(T):
                sp.wait_ge(fin_ready, t + 1)
                sp.dma_start(out_rows[:, t, :], fin[:, t % 2, :]).then_inc(out_stored[t % 2], 16)
            for n in range(2):
                sp.wait_ge(out_stored[n], 16 * T // 2)

        @block.gpsimd
        def _(pool):
            pool.wait_ge(x1_stored, 16 * T)
            pool.wait_ge(token_ready, 1)

            for m in range(SLOTS):
                if m >= 4:
                    pool.wait_ge(xt_done, m - 3)
                pool.indirect_dma_start(
                    xg[:, m % 4, :], None, x1_dram.ap(),
                    bass.IndirectOffsetOnAxis(ap=token[:, m:m + 1], axis=0)).then_inc(gath[m % 4], 16)
            pool.wait_ge(slots_ready, 1)
            for j in range(4):
                pool.wait_ge(y_stored[j], 16 * SLOTS // 4)
            for t in range(T):
                for k in range(K):
                    n = t * K + k
                    pool.indirect_dma_start(
                        yg[:, n, :], None, y_rows,
                        bass.IndirectOffsetOnAxis(ap=slot_i[:, n:n + 1], axis=0)).then_inc(yg_in[t], 16)

        @block.tensor
        def _(pe):
            pe.wait_ge(ld_c, 16)
            for b in range(B):
                for c in range(DC):
                    for i in range(TB):
                        t = b * TB + i
                        pe.wait_ge(z_ready, t + 1)
                        mm = pe.transpose(bank[2 * b + c][:, i * P:(i + 1) * P],
                                          z_sb[:, t, c * P:(c + 1) * P], ident)
                    mm.then_inc(zt_done, 1)

            def expand_mm(n, rows, parts, lhs, rhs):
                if n >= 4:
                    pe.wait_ge(*released(n - 4))
                for c in range(DC):
                    mm = pe.matmul(bank[4 + n % 4][0:parts, 0:rows], lhs(c), rhs(c),
                                   start=(c == 0), stop=(c == DC - 1))
                mm.then_inc(ex_done, 1)

            pe.wait_ge(ld_ex, 16)
            for b in range(B):
                pe.wait_ge(h_ready, DC * (b + 1))
                toks = slice(b * S, (b + 1) * S)
                n = b * JOBS
                for j, (at, width) in enumerate([(X_Q, QK), (X_K, QK), (X_PRE, P), (X_LIN, P),
                                                 (X_PRE + P, P), (X_LIN + P, P)]):
                    expand_mm(n + j, S, width, lambda c: ex_w[:, c, at:at + width], lambda c: hT[:, c, toks])
                for i in range(TB):
                    t = b * TB + i
                    expand_mm(n + 6 + i, 2 * D, P, lambda c: hT[:, c, t * P:(t + 1) * P],
                              lambda c: ex_w[:, c, X_VAL:X_VAL + 2 * D])

            def scores(t):
                b, i = divmod(t, TB)
                pe.wait_ge(qk_ready, 2 * (b + 1))
                if t >= 2:
                    pe.wait_ge(smax_ready, t - 1)
                pe.matmul(bank[t % 2][:, 0:(i + 1) * P], qT[:, t * P:(t + 1) * P],
                          kT[:, b * S:b * S + (i + 1) * P], start=True, stop=True).then_inc(sc_done, 1)

            def turn_probs(t):
                pe.wait_ge(p_ready, t + 1)
                if t >= 1:
                    pe.wait_ge(pt_ready, t)
                for j in range(t % TB + 1):
                    mm = pe.transpose(bank[2][:, j * P:(j + 1) * P], p_sb[:, t % 2, j * P:(j + 1) * P], ident)
                mm.then_inc(pt_done, 1)

            def attend(t):
                b, i = divmod(t, TB)
                pe.wait_ge(pt_ready, t + 1)
                pe.wait_ge(geglu_ready, 6 * b + 3 + i)
                if t == 0:
                    pe.wait_ge(*released(2 * JOBS - 4))
                else:
                    pe.wait_ge(at_ready, t)
                for v in range(2):
                    for j in range(i + 1):
                        mm = pe.matmul(bank[4][:, v * P:(v + 1) * P], val[:, b * TB + j, v * P:(v + 1) * P],
                                       pT[:, j * P:(j + 1) * P], start=(j == 0), stop=(j == i))
                mm.then_inc(av_done, 1)

            def project_mm(t):
                pe.wait_ge(at_ready, t + 1)
                pe.wait_ge(ld_pj, 32)
                if t == 0:
                    pe.wait_ge(*released(2 * JOBS - 3))
                else:
                    pe.wait_ge(y1_ready, t)
                for c in range(2 * DC):
                    lhs = locT[:, c, t * P:(t + 1) * P] if c < DC else aT[:, t % 2, (c - DC) * P:(c - DC + 1) * P]
                    mm = pe.matmul(bank[5][:, 0:D], lhs, pj_w[:, c, :], start=(c == 0), stop=(c == 2 * DC - 1))
                mm.then_inc(pj_done, 1)

            def turn_x1(t):
                pe.wait_ge(x1_ready, t + 1)
                if t == 0:
                    pe.wait_ge(*released(2 * JOBS - 2))
                else:
                    pe.wait_ge(x1t_ready, t)
                for c in range(DC):
                    mm = pe.transpose(bank[6][:, c * P:(c + 1) * P], x1[:, t, c * P:(c + 1) * P], ident)
                mm.then_inc(x1t_done, 1)

            def logits(t):
                b, i = divmod(t, TB)
                pe.wait_ge(x1t_ready, t + 1)
                if t == 0:
                    pe.wait_ge(*released(2 * JOBS - 1))
                for c in range(DC):
                    mm = pe.matmul(bank[7 if b else 3][:, i * E:(i + 1) * E], x1T[:, c, t * P:(t + 1) * P],
                                   rt_w[:, c, :], start=(c == 0), stop=(c == DC - 1))
                mm.then_inc(lg_done, 1)

            for s in range(T + LAG_XT):
                for lag, stage in ((0, scores), (LAG_PT, turn_probs), (LAG_AV, attend),
                                   (LAG_PJ, project_mm), (LAG_XT, turn_x1), (LAG_XT, logits)):
                    if 0 <= s - lag < T:
                        stage(s - lag)

            GU, HT, DN = (2, 4), (5, 6), (3, 7)

            def turn_rows(m, j):
                pe.wait_ge(gath[j], m_count(m, j))
                if not (isinstance(m, int) and m < 2):
                    pe.wait_ge(xt_ready, m - 1)
                for c in range(DC):
                    mm = pe.transpose(bank[j % 2][:, c * P:(c + 1) * P], xg[:, j, c * P:(c + 1) * P], ident)
                mm.then_inc(xt_done, 1)

            def m_count(m, j):
                return 16 * (m // 4 + 1) if isinstance(m, int) else 4 * m + (16 - 4 * j)

            def gate_up_mm(s, j, lhs, rhs):
                if not (isinstance(s, int) and s < 2):
                    pe.wait_ge(clipped, s - 1)
                for c in range(DC):
                    mm = pe.matmul(bank[GU[j % 2]][:, 0:2 * I], lhs(c), rhs(c), start=(c == 0), stop=(c == DC - 1))
                mm.then_inc(gu_done, 1)

            def turn_h(s, j):
                pe.wait_ge(hh_ready, s + 1)
                if not (isinstance(s, int) and s < 2):
                    pe.wait_ge(ht_ready, s - 1)
                pe.transpose(bank[HT[j % 2]][:, 0:P], hh[:, j % 2, :], ident).then_inc(ht_done, 1)

            def down_mm(s, j, w):
                pe.wait_ge(ht_ready, s + 1)
                if not (isinstance(s, int) and s < 2):
                    pe.wait_ge(y_ready, s - 1)
                pe.matmul(bank[DN[j % 2]][:, 0:D], hTs[:, j % 2, :], w, start=True, stop=True).then_inc(dn_done, 1)

            def rank_mm(half):
                pe.wait_ge(oh_ready, half + 1)
                if half == 0:
                    pe.wait_ge(smax_ready, T - 1)
                for t in range(half * TB, (half + 1) * TB):
                    for k in range(K):
                        first = t == 0 and k == 0
                        n = T - t
                        rhs = oh[:, t, k, :].unsqueeze(1).to_broadcast([P, n, E])
                        pe.matmul(bank[0][:, (t + 1) * E:(T + 1) * E], ones16, rhs,
                                  start=first, stop=False, skip_group_check=True)
                        mm = pe.matmul(bank[0][:, t * E:(t + 1) * E], before16, oh[:, t, k, :],
                                       start=False, stop=(t == T - 1 and k == K - 1), skip_group_check=True)
                if half == 1:
                    mm.then_inc(pos_done, 1)

            def starts_mm():
                pe.wait_ge(ntcol_ready, 1)
                pe.wait_ge(smax_ready, T)
                pe.matmul(bank[1][:, 0:2 * E], ntcol[:, :].to_broadcast([E, P]), cst[0:E, C_TRI:C_TRI + 2 * E],
                          start=True, stop=True).then_inc(start_done, 1)

            def tile_experts_mm():
                pe.wait_ge(te_ready, 1)
                pe.matmul(bank[1][0:1, 0:P], te_col[:, :], ident, start=True, stop=True).then_inc(ter_done, 1)

            def token_list_mm():
                pe.wait_ge(ohr_ready, 1)
                for n in range(T * K):
                    mm = pe.matmul(bank[0][:, 0:SLOTS], ohr[:, n * P:(n + 1) * P], idt[:, n, :],
                                   start=(n == 0), stop=(n == T * K - 1))
                mm.then_inc(list_done, 1)

            def shared_gu(t):
                if t == 0:
                    pe.wait_ge(ld_sh, 32)
                    pe.wait_ge(pt_ready, T)
                    pe.wait_ge(at_ready, T)
                gate_up_mm(t, t, lambda c: x1T[:, c, t * P:(t + 1) * P], lambda c: w_gu[:, E, c, :])

            rank_mm(0)
            for s in range(T):
                shared_gu(s)
                if s >= 1:
                    if s == 1:
                        pe.wait_ge(x1t_ready, T)
                    turn_h(s - 1, s - 1)
                if s == 1:
                    rank_mm(1)
                if s == 3:
                    starts_mm()
                if s == 4:
                    tile_experts_mm()
                if s >= 2:
                    if s == 2:
                        pe.wait_ge(r_dve, 2)
                    down_mm(s - 2, s - 2, w_dn[:, E, :])
            token_list_mm()
            pe.wait_ge(te_loaded, 1)
            pe.wait_ge(ld_w, 16 * 16)
            pe.wait_ge(token_ready, 1)

            def expert_of(col):
                return pe.value_load(te_row[0:1, col], min_val=0, max_val=E - 1)

            def step(m, j, static):
                s = m + T
                if not (static and m + 1 >= SLOTS):
                    turn_rows(m + 1, (j + 1) % 4)
                if not (static and m >= SLOTS):
                    e = expert_of(slice(m, m + 1) if static else bass.ds(m, 1))
                    pe.wait_ge(xt_ready, m + 1)
                    gate_up_mm(s, j, lambda c: xT[:, j % 2, c * P:(c + 1) * P],
                               lambda c: w_gu[:, bass.ds(e, 1), c, :].rearrange("p o n -> p (o n)"))
                if not (static and m - 1 >= SLOTS):
                    turn_h(s - 1, j + 3)
                if static and m < 2:
                    down_mm(s - 2, j + 2, w_dn[:, E, :])
                else:
                    e = expert_of(slice(m - 2, m - 1) if static else bass.ds(m - 2, 1))
                    down_mm(s - 2, j + 2, w_dn[:, bass.ds(e, 1), :].rearrange("p o n -> p (o n)"))

            turn_rows(0, 0)
            for m in range(4):
                step(m, m, True)
            with pe.Fori(1, SLOTS // 4 - 1) as n:
                for j in range(4):
                    step(4 * n + j, j, False)
            for m in range(SLOTS - 4, SLOTS + 2):
                step(m, m % 4, True)

        @block.vector
        def _(dve):
            steps = [0]

            def link(ins):
                steps[0] += 1
                ins.then_inc(vec, 1)
                dve.wait_ge(vec, steps[0])

            def polish(cols):
                v, r, a, c = mv[:, cols, 1:2], rs[:, cols].unsqueeze(2), nt[:, cols, 0:1], nt[:, cols, 1:2]
                link(dve.scalar_tensor_tensor(out=a, in0=v, scalar=EPS, in1=r, op0=ALU.add, op1=ALU.mult))
                link(dve.tensor_tensor(c, a, r, ALU.mult))
                link(dve.tensor_scalar(a, c, -0.5, 1.5, ALU.mult, ALU.add))
                link(dve.tensor_tensor(r, a, r, ALU.mult))

            for b in range(B):
                dve.wait_ge(ld_x[b], 16)
                for t in range(b * TB, (b + 1) * TB):
                    ins = dve.bn_stats(bst[:, t, :], x_sb[:, t, :])
                link(ins)
                for t in range(b * TB, (b + 1) * TB):
                    ins = dve.bn_aggr(mv[:, t, :], bst[:, t, :])
                ins.then_inc(var_ready, 1)
            for b in range(B):
                dve.wait_ge(rstd_ready, b + 1)
                dve.wait_ge(var_ready, b + 1)
                polish(slice(b * TB, (b + 1) * TB))
                for t in range(b * TB, (b + 1) * TB):
                    dve.tensor_scalar(z_sb[:, t, :], x_sb[:, t, :], mv[:, t, 0:1], rs[:, t:t + 1],
                                      ALU.subtract, ALU.mult).then_inc(z_ready, 1)
            dve.wait_ge(ld_c, 16)
            dve.tensor_copy(sc16[:, :], cst[:, 0:4 * P]).then_inc(consts_ready, 1)
            dve.wait_ge(pos_ready, 1)
            link(dve.scalar_tensor_tensor(out=pb[:, 3:4], in0=sml[:, 2 * DC:2 * DC + 1], scalar=0.0,
                                          in1=pb[:, 2:3], op0=ALU.max, op1=ALU.add))
            link(dve.scalar_tensor_tensor(out=bmat[:, :], in0=cst[:, C_REL:C_REL + S], scalar=pb[:, 3:4],
                                          in1=cst[:, C_MASK:C_MASK + S], op0=ALU.mult, op1=ALU.add))
            for b in range(B):
                for c in range(2):
                    dve.wait_ge(ex_done, b * JOBS + 4 + 2 * c)
                    dve.wait_ge(gelu_ready, 6 * b + c + 1)
                    dve.tensor_tensor(locT[:, c, b * S:(b + 1) * S], bank[4 + (b * JOBS + 3 + 2 * c) % 4][:, :],
                                      gl[:, c, :], ALU.mult).then_inc(geglu_ready, 1)
                for i in range(TB):
                    dve.wait_ge(gelu_ready, 6 * b + 3 + i)
                    dve.tensor_tensor(val[:, b * TB + i, :], bank[4 + (b * JOBS + 6 + i) % 4][:, 0:D],
                                      gv[:, i % 2, :], ALU.mult).then_inc(geglu_ready, 1)

            def row_max(t):
                i = t % TB
                w = (i + 1) * P
                dve.wait_ge(sc_done, t + 1)
                if t >= 2:
                    dve.wait_ge(exp_ready, t - 1)
                link(dve.tensor_tensor_reduce(s_sb[:, t % 2, 0:w], bank[t % 2][:, 0:w], bmat[:, S - w:S], 1.0,
                                              3.0 * NEG, ALU.add, ALU.max, mxs[:, t, 0:1]))
                dve.tensor_scalar(mxs[:, t, 1:2], mxs[:, t, 0:1], -1.0, None, ALU.mult).then_inc(smax_ready, 1)

            def normalize_probs(t):
                w = (t % TB + 1) * P
                dve.wait_ge(exp_ready, t + 1)
                link(dve.reciprocal(mxs[:, t, 3:4], mxs[:, t, 2:3]))
                dve.tensor_scalar(p_sb[:, t % 2, 0:w], p_sb[:, t % 2, 0:w], mxs[:, t, 3:4], None,
                                  ALU.mult).then_inc(p_ready, 1)

            def residual(t):
                dve.wait_ge(pj_done, t + 1)
                if t >= 2:
                    dve.wait_ge(x1_ready, t - 1)
                link(dve.scalar_tensor_tensor(out=y1[:, t % 2, :], in0=x_sb[:, t, :], scalar=2.0,
                                              in1=bank[5][:, 0:D], op0=ALU.mult, op1=ALU.add))
                link(dve.bn_stats(bst[:, t, :], y1[:, t % 2, :]))
                dve.bn_aggr(mv[:, t, :], bst[:, t, :]).then_inc(y1_ready, 1)

            def finish_x1(t):
                dve.wait_ge(rstd2_ready, t + 1)
                polish(slice(t, t + 1))
                dve.wait_ge(zt_done, B * DC)
                dve.tensor_scalar(x1[:, t, :], y1[:, t % 2, :], mv[:, t, 0:1], rs[:, t:t + 1],
                                  ALU.subtract, ALU.mult).then_inc(x1_ready, 1)

            def softplus_sqrt(h):
                ts = slice(h * TB, (h + 1) * TB)
                l, a, e, u, d, q = lg[:, ts, :], ra[:, ts, :], re_[:, ts, :], rb[:, ts, :], rc[:, ts, :], score[:, ts, :]
                one = sel[:, ts, :]
                dve.wait_ge(lg_done, (h + 1) * TB)
                dve.tensor_copy(l, bank[7 if h else 3][:, 0:TB * E].rearrange("p (t e) -> p t e", e=E)).then_inc(r_dve, 1)
                dve.wait_ge(r_act, 3 * h + 1)
                dve.tensor_scalar(u, e, 1.0, None, ALU.add).then_inc(r_dve, 1)
                dve.wait_ge(r_dve, 3 * h + 2)
                link(dve.tensor_scalar(d, u, -1.0, None, ALU.add))
                link(dve.tensor_scalar(one, d, 0.0, None, ALU.is_equal))
                dve.wait_ge(r_act, 3 * h + 2)
                link(dve.tensor_tensor(d, d, one, ALU.add))
                link(dve.tensor_tensor(a, a, one, ALU.add))
                link(dve.reciprocal(d, d))
                link(dve.tensor_tensor(a, a, e, ALU.mult))
                link(dve.tensor_tensor(a, a, d, ALU.mult))
                link(dve.scalar_tensor_tensor(out=a, in0=l, scalar=0.0, in1=a, op0=ALU.max, op1=ALU.add))
                dve.tensor_scalar(a, a, 2.0 ** -110, None, ALU.max).then_inc(r_dve, 1)
                dve.wait_ge(r_dve, 3 * h + 3)
                dve.wait_ge(r_act, 3 * h + 3)
                link(dve.reciprocal(d, u))
                link(dve.tensor_tensor(d, d, a, ALU.mult))
                link(dve.tensor_tensor(d, d, u, ALU.add))
                link(dve.tensor_scalar(q, d, 0.5, None, ALU.mult))

            def choose(h):
                ts = slice(h * TB, (h + 1) * TB)
                link(dve.tensor_tensor(sel[:, ts, :], score[:, ts, :],
                                       bias_e[:, :].unsqueeze(1).to_broadcast([P, TB, E]), ALU.add))
                for t in range(h * TB, (h + 1) * TB):
                    ins = dve.max(top[:, t, :], sel[:, t, :])
                link(ins)
                for t in range(h * TB, (h + 1) * TB):
                    ins = dve.max_index(topi[:, t, :], top[:, t, :], sel[:, t, :])
                link(ins)
                link(dve.tensor_copy(topf[:, ts, :], topi[:, ts, 0:K]))
                dve.tensor_tensor(oh[:, ts, :, :],
                                  iota16[:, 0:E].unsqueeze(1).unsqueeze(1).to_broadcast([P, TB, K, E]),
                                  topf[:, ts, :].unsqueeze(3).to_broadcast([P, TB, K, E]),
                                  ALU.is_equal).then_inc(oh_ready, 1)

            def shares():
                dve.wait_ge(oh_ready, 2)
                link(dve.tensor_tensor(prod[:, :, :, :], oh[:, :, :, :],
                                       score[:, :, :].unsqueeze(2).to_broadcast([P, T, K, E]), ALU.mult))
                link(dve.tensor_reduce(pk[:, :, :], prod[:, :, :, :], AX, ALU.add))
                link(dve.tensor_reduce(psum_k[:, :, 0:1], pk[:, :, :], AX, ALU.add))
                link(dve.tensor_scalar(psum_k[:, :, 0:1], psum_k[:, :, 0:1], 1e-20, None, ALU.add))
                link(dve.reciprocal(psum_k[:, :, 1:2], psum_k[:, :, 0:1]))
                link(dve.tensor_tensor(pk[:, :, :], pk[:, :, :], psum_k[:, :, 1:2].to_broadcast([P, T, K]), ALU.mult))

            def count_tiles():
                dve.wait_ge(pos_done, 1)
                link(dve.tensor_scalar(ntile_i[:, :], bank[0][:, T * E:(T + 1) * E], float(P - 1), None, ALU.add))
                link(dve.tensor_scalar(ntile_j[:, :], ntile_i[:, :], 7, None, ALU.logical_shift_right))
                link(dve.tensor_copy(ntile[:, :], ntile_j[:, :]))
                dve.tensor_tensor_reduce(ntd[:, :], ntile[0:E, :], ident[0:E, 0:E], 1.0, 0.0, ALU.mult, ALU.add,
                                         ntcol[:, :]).then_inc(ntcol_ready, 1)

            def tile_experts():
                dve.wait_ge(start_done, 1)
                dve.tensor_scalar(base[:, :], bank[1][:, 0:E], float(P), None, ALU.mult)
                link(dve.tensor_copy(ends[:, :], bank[1][:, E:2 * E]))
                link(dve.tensor_scalar(ends[:, :], ends[:, :], cst[:, C_PID:C_PID + 1], None, ALU.is_le, ALU.add,
                                       accum_out=te_col[:, :]))
                dve.tensor_scalar(te_col[:, :], te_col[:, :], float(E - 1), None, ALU.min).then_inc(te_ready, 1)

            def find_slots():
                link(dve.tensor_tensor(posb[:, :, :], bank[0][:, 0:T * E].rearrange("p (t e) -> p t e", e=E),
                                       base[:, :].unsqueeze(1).to_broadcast([P, T, E]), ALU.add))
                link(dve.tensor_tensor(prod[:, :, :, :], oh[:, :, :, :],
                                       posb[:, :, :].unsqueeze(2).to_broadcast([P, T, K, E]), ALU.mult))
                link(dve.tensor_reduce(slot_f[:, :].rearrange("p (t k) -> p t k", k=K), prod[:, :, :, :], AX, ALU.add))
                link(dve.tensor_copy(slot_i[:, :], slot_f[:, :]))
                dve.tensor_scalar(slot_t[:, 0, :], slot_i[:, :], 7, None, ALU.logical_shift_right)
                link(dve.tensor_scalar(slot_t[:, 1, :], slot_i[:, :], P - 1, None, ALU.bitwise_and))
                link(dve.tensor_copy(slot_r[:, :, :], slot_t[:, :, :]))

            def expert_rows():
                dve.wait_ge(ter_done, 1)
                dve.tensor_copy(te_row[:, :], bank[1][0:1, 0:SLOTS]).then_inc(te_loaded, 1)

            def list_operands(n0, n1):
                dve.wait_ge(ex_done, 2 * JOBS)
                for n in range(n0, n1):
                    dve.tensor_scalar(ohr[:, n * P:(n + 1) * P], iota16, slot_r[:, 1, n:n + 1], None, ALU.is_equal)
                    ins = dve.tensor_scalar(idt[:, n, :], iota16[:, 0:SLOTS], slot_r[:, 0, n:n + 1],
                                            cst[:, C_TOK + n // K:C_TOK + n // K + 1], ALU.is_equal, ALU.mult)
                if n1 == T * K:
                    ins.then_inc(ohr_ready, 1)

            def token_list():
                dve.wait_ge(list_done, 1)
                dve.tensor_copy(token[:, :], bank[0][:, 0:SLOTS]).then_inc(token_ready, 1)

            def clip(s, j):
                dve.wait_ge(gu_done, s + 1)
                if not (isinstance(s, int) and s < 2):
                    dve.wait_ge(hh_ready, s - 1)
                dve.tensor_scalar(gu[:, j % 2, :], bank[(2, 4)[j % 2]][:, 0:2 * I], ALPHA, -ALPHA,
                                  ALU.min, ALU.max).then_inc(clipped, 1)

            def copy_hT(s, j):
                dve.wait_ge(ht_done, s + 1)
                if not (isinstance(s, int) and s < 2):
                    dve.wait_ge(dn_done, s - 1)
                dve.tensor_copy(hTs[:, j % 2, :], bank[(5, 6)[j % 2]][:, 0:P]).then_inc(ht_ready, 1)

            def gate_times_up(s, j):
                dve.wait_ge(silu_ready, s + 1)
                if not (isinstance(s, int) and s < 2):
                    dve.wait_ge(ht_done, s - 1)
                dve.tensor_tensor(hh[:, j % 2, :], sg[:, j % 2, :], gu[:, j % 2, I:2 * I], ALU.mult).then_inc(hh_ready, 1)

            for s in range(T + LAG_XT):
                if 0 <= s - 1 < T:
                    normalize_probs(s - 1)
                if s < T:
                    row_max(s)
                if 0 <= s - LAG_PJ < T:
                    residual(s - LAG_PJ)
                if 0 <= s - LAG_FIN < T:
                    finish_x1(s - LAG_FIN)
                if s == 2 * TB + 2:
                    softplus_sqrt(0)
                    dve.wait_ge(consts_ready, 1)
                    choose(0)
            softplus_sqrt(1)
            choose(1)

            def shared_step(s):
                if s < T:
                    clip(s, s)
                if s >= 1:
                    copy_hT(s - 1, s - 1)
                if s < T:
                    gate_times_up(s, s)

            shared_step(0)
            shared_step(1)
            count_tiles()
            shared_step(2)
            shared_step(3)
            tile_experts()
            find_slots()
            shared_step(4)
            expert_rows()
            list_operands(0, T * K // 2)
            shared_step(5)
            list_operands(T * K // 2, T * K)
            shared_step(6)
            shared_step(7)
            token_list()
            shares()
            dve.drain().then_inc(slots_ready, 1)

            def step(m, j, static):
                s = m + T
                if not (static and m >= SLOTS):
                    clip(s, j)
                copy_hT(s - 1, j + 3)
                if not (static and m >= SLOTS):
                    gate_times_up(s, j)

            step(0, 0, True)
            with dve.Fori(0, SLOTS // 2 - 1) as n:
                for j in range(2):
                    step(2 * n + (j + 1), j + 1, False)
            step(SLOTS - 1, SLOTS - 1, True)
            step(SLOTS, SLOTS, True)

            def combine(t):
                dve.wait_ge(yg_in[t], 16 * K)
                if t >= 2:
                    dve.wait_ge(fin_ready, t - 1)
                a = acc[:, t % 2, :]
                link(dve.scalar_tensor_tensor(out=a, in0=yg[:, t * K, :], scalar=pk[:, t, 0:1], in1=shared[:, t, :],
                                              op0=ALU.mult, op1=ALU.add))
                for k in range(1, K):
                    link(dve.scalar_tensor_tensor(out=a, in0=yg[:, t * K + k, :], scalar=pk[:, t, k:k + 1], in1=a,
                                                  op0=ALU.mult, op1=ALU.add))
                link(dve.tensor_tensor(a, a, x1[:, t, :], ALU.add))
                link(dve.bn_stats(bst[:, t, :], a))
                dve.bn_aggr(mv[:, t, :], bst[:, t, :]).then_inc(var3_ready, 1)

            def finish(t):
                dve.wait_ge(var3_ready, t + 1)
                dve.wait_ge(rstd3_ready, t + 1)
                polish(slice(t, t + 1))
                if t >= 2:
                    dve.wait_ge(out_stored[t % 2], 16 * (t // 2))
                dve.tensor_scalar(fin[:, t % 2, :], acc[:, t % 2, :], mv[:, t, 0:1], rs[:, t:t + 1],
                                  ALU.subtract, ALU.mult).then_inc(fin_ready, 1)

            for t in range(T + 1):
                if t < T:
                    combine(t)
                if t >= 1:
                    finish(t - 1)

        @block.scalar
        def _(act):
            steps = [0]

            def link(ins):
                steps[0] += 1
                ins.then_inc(act_, 1)
                act.wait_ge(act_, steps[0])

            def rstd(cols, ready):
                r = rs[:, cols].unsqueeze(2)
                act.activation(r, mv[:, cols, 1:2], ACT.Ln, bias=sml_eps).then_inc(act_, 1)
                steps[0] += 1
                act.wait_ge(act_, steps[0])
                act.activation(r, r, ACT.Exp, scale=-0.5).then_inc(ready, 1)

            sml_eps = EPS
            for b in range(B):
                act.wait_ge(var_ready, b + 1)
                rstd(slice(b * TB, (b + 1) * TB), rstd_ready)
            act.wait_ge(ld_s, 32)
            link(act.activation(pb[:, 0:1], sml[:, 2 * DC:2 * DC + 1], ACT.Abs))
            link(act.activation(pb[:, 1:2], pb[:, 0:1], ACT.Exp, scale=-1.0))
            act.activation(pb[:, 2:3], pb[:, 1:2], ACT.Ln, bias=1.0).then_inc(pos_ready, 1)
            for b in range(B):
                for c in range(DC):
                    act.wait_ge(zt_done, b * DC + c + 1)
                    act.activation(hT[:, c, b * S:(b + 1) * S], bank[2 * b + c][:, :], ACT.Identity,
                                   bias=sml[:, DC + c:DC + c + 1], scale=sml[:, c:c + 1]).then_inc(h_ready, 1)
            for b in range(B):
                n = b * JOBS
                cols = slice(b * S, (b + 1) * S)
                act.wait_ge(ex_done, n + 1)
                act.activation(qT[:, cols], bank[4 + n % 4][0:QK, :], ACT.Copy, scale=float(QK) ** -0.5).then_inc(qk_ready, 1)
                act.wait_ge(ex_done, n + 2)
                act.activation(kT[:, cols], bank[4 + (n + 1) % 4][0:QK, :], ACT.Copy).then_inc(qk_ready, 1)
                for c in range(2):
                    act.wait_ge(ex_done, n + 3 + 2 * c)
                    if b:
                        act.wait_ge(geglu_ready, 6 * (b - 1) + c + 1)
                    act.activation(gl[:, c, :], bank[4 + (n + 2 + 2 * c) % 4][:, :], ACT.Gelu).then_inc(gelu_ready, 1)
                for i in range(TB):
                    act.wait_ge(ex_done, n + 7 + i)
                    if i >= 2:
                        act.wait_ge(geglu_ready, 6 * b + 3 + i - 2)
                    elif b:
                        act.wait_ge(geglu_ready, 6 * (b - 1) + 3 + TB - 2 + i)
                    act.activation(gv[:, i % 2, :], bank[4 + (n + 6 + i) % 4][:, D:2 * D], ACT.Gelu).then_inc(gelu_ready, 1)

            def exps(t):
                w = (t % TB + 1) * P
                act.wait_ge(smax_ready, t + 1)
                if t >= 2:
                    act.wait_ge(pt_done, t - 1)
                act.activation(p_sb[:, t % 2, 0:w], s_sb[:, t % 2, 0:w], ACT.Exp, bias=mxs[:, t, 1:2],
                               accum_out=mxs[:, t, 2:3]).then_inc(exp_ready, 1)

            def copy_pT(t):
                w = (t % TB + 1) * P
                act.wait_ge(pt_done, t + 1)
                if t >= 1:
                    act.wait_ge(av_done, t)
                act.activation(pT[:, 0:w], bank[2][:, 0:w], ACT.Copy).then_inc(pt_ready, 1)

            def copy_aT(t):
                act.wait_ge(av_done, t + 1)
                if t >= 2:
                    act.wait_ge(pj_done, t - 1)
                act.activation(aT[:, t % 2, :], bank[4][:, 0:D], ACT.Copy).then_inc(at_ready, 1)

            def rstd2(t):
                act.wait_ge(y1_ready, t + 1)
                rstd(slice(t, t + 1), rstd2_ready)

            def copy_x1T(t):
                act.wait_ge(x1t_done, t + 1)
                act.wait_ge(ex_done, 2 * JOBS)
                act.activation(x1T[:, :, t * P:(t + 1) * P], bank[6][:, 0:D].rearrange("p (c n) -> p c n", c=DC),
                               ACT.Copy).then_inc(x1t_ready, 1)

            def route(h):
                ts = slice(h * TB, (h + 1) * TB)
                act.wait_ge(r_dve, 3 * h + 1)
                link(act.activation(ra[:, ts, :], lg[:, ts, :], ACT.Abs))
                act.activation(re_[:, ts, :], ra[:, ts, :], ACT.Exp, scale=-1.0).then_inc(r_act, 1)
                act.wait_ge(r_dve, 3 * h + 2)
                act.activation(ra[:, ts, :], rb[:, ts, :], ACT.Ln).then_inc(r_act, 1)
                act.wait_ge(r_dve, 3 * h + 3)
                link(act.activation(rb[:, ts, :], ra[:, ts, :], ACT.Ln, scale=2.0 ** SQ_UP))
                act.activation(rb[:, ts, :], rb[:, ts, :], ACT.Exp, scale=0.5, bias=-0.5 * SQ_UP * LN2).then_inc(r_act, 1)

            for s in range(T + LAG_XT):
                if s < T:
                    exps(s)
                for lag, stage in ((LAG_PT, copy_pT), (LAG_AV, copy_aT), (LAG_PJ, rstd2), (LAG_XT, copy_x1T)):
                    if 0 <= s - lag < T:
                        stage(s - lag)
                if s == 2 * TB + 2:
                    route(0)
            route(1)

            def copy_xT(m, j):
                act.wait_ge(xt_done, m + 1)
                if not (isinstance(m, int) and m < 2):
                    act.wait_ge(gu_done, m + T - 1)
                act.activation(xT[:, j % 2, :], bank[j % 2][:, 0:D], ACT.Copy).then_inc(xt_ready, 1)

            def silu(s, j):
                act.wait_ge(clipped, s + 1)
                if not (isinstance(s, int) and s < 2):
                    act.wait_ge(hh_ready, s - 1)
                act.activation(sg[:, j % 2, :], gu[:, j % 2, 0:I], ACT.Silu).then_inc(silu_ready, 1)

            def copy_y(s, j, dst):
                act.wait_ge(dn_done, s + 1)
                act.activation(dst, bank[(3, 7)[j % 2]][:, 0:D], ACT.Copy).then_inc(y_ready, 1)

            for s in range(T):
                silu(s, s)
                if s >= 2:
                    copy_y(s - 2, s - 2, shared[:, s - 2, :])

            def step(m, j, static):
                s = m + T
                if not (static and m + 1 >= SLOTS):
                    copy_xT(m + 1, j + 1)
                if not (static and m >= SLOTS):
                    silu(s, j)
                if static and m < 2:
                    copy_y(s - 2, j + 2, shared[:, s - 2, :])
                    return
                if not (static and m < 6):
                    act.wait_ge(y_stored[(j + 2) % 4], 16 * ((m - 2) // 4) if static else 4 * m - (8 + 4 * ((j + 2) % 4)))
                copy_y(s - 2, j + 2, y_sb[:, (j + 2) % 4, :])

            copy_xT(0, 0)
            for m in range(8):
                step(m, m % 4, True)
            with act.Fori(2, SLOTS // 4 - 1) as n:
                for j in range(4):
                    step(4 * n + j, j, False)
            for m in range(SLOTS - 4, SLOTS + 2):
                step(m, m % 4, True)

            for t in range(T):
                act.wait_ge(var3_ready, t + 1)
                rstd(slice(t, t + 1), rstd3_ready)


def _constants(np):
    c = np.zeros((P, NCONST), np.float32)
    p = np.arange(P)[:, None]
    n = np.arange(P)[None, :]
    c[:, C_ID:C_ID + P] = p == n
    c[:, C_LT:C_LT + P] = p < n
    c[:, C_ONE:C_ONE + P] = 1.0
    c[:, C_IOTA:C_IOTA + P] = n
    rel = np.arange(S)[None, :] - (S - P) - p
    c[:, C_REL:C_REL + S] = np.minimum(rel, 0)
    c[:, C_MASK:C_MASK + S] = np.where(rel > 0, NEG, 0.0)
    c[:, C_TOK:C_TOK + T] = np.arange(T)[None, :] * P + p
    c[:, C_PID:C_PID + 1] = p
    e = np.arange(E)[None, :]
    c[:, C_TRI:C_TRI + E] = p < e
    c[:, C_TRI + E:C_TRI + 2 * E] = p <= e
    return c


def kernel(**inputs):
    import numpy as np
    import concourse.bacc as bacc
    from concourse.bass_utils import run_bass_kernel_spmd as run

    a = {k: np.asarray(v) for k, v in inputs.items()}

    def chunked(w, lead):
        return w.T.reshape(lead, P, w.shape[0]).transpose(1, 0, 2)

    ex = a["L0_attn_expand"]
    loc, value = 2 * QK, 2 * QK + LOC
    pre = 2 * QK + 2 * D
    ex = np.concatenate([ex[0:2 * QK], ex[loc:loc + D], ex[pre:pre + D], ex[value:value + D], ex[pre + D:pre + 2 * D]])
    gate = np.concatenate([a["L0_ffn_gate_w"], a["L0_ffn_shared_gate_w"][None]])
    up = np.concatenate([a["L0_ffn_up_w"], a["L0_ffn_shared_up_w"][None]])
    dn = np.concatenate([a["L0_ffn_down_w"], a["L0_ffn_shared_down_w"][None]])
    gu = np.concatenate([gate, up], axis=1)
    gu = gu.transpose(2, 0, 1).reshape(DC, P, EW, 2 * I).transpose(1, 2, 0, 3)
    small = np.concatenate([a["L0_attn_ln_gamma"].reshape(DC, P).T, a["L0_attn_ln_beta"].reshape(DC, P).T,
                            np.broadcast_to(a["L0_attn_pos_mult"].reshape(1, 1), (P, 1))], axis=1)
    arrays = {
        "x": a["L0_attn_x"],
        "consts": _constants(np),
        "small": small,
        "rbias": a["L0_ffn_expert_bias"].reshape(1, E),
        "expand": chunked(ex, DC),
        "project": chunked(a["L0_attn_project"], 2 * DC),
        "router": chunked(a["L0_ffn_router_w"], DC),
        "gate_up": gu,
        "down": dn.transpose(2, 0, 1),
    }
    arrays = {k: np.ascontiguousarray(v) for k, v in arrays.items()}
    nc = bacc.Bacc("TRN2", target_bir_lowering=False, num_devices=1)
    args = {k: nc.dram_tensor(f"in_{k}", v.shape, mybir.dt.from_np(v.dtype), kind="ExternalInput").ap()
            for k, v in arrays.items()}
    args["out"] = nc.dram_tensor("out_0", (B, S, D), F32, kind="ExternalOutput").ap()
    attn_moe_program(nc, **args)
    r = run(nc, [{f"in_{k}": v for k, v in arrays.items()}], core_ids=[0])
    return r.results[0]["out_0"]
```

```python
from contextlib import ExitStack
from itertools import islice

import concourse.bass as bass
from concourse import mybir

F32 = mybir.dt.float32
F16 = mybir.dt.float16
I32 = mybir.dt.int32
U32 = mybir.dt.uint32
ALU = mybir.AluOpType
ACT = mybir.ActivationFunctionType
AX = mybir.AxisListType.X

P = 128
B, S, D = 2, 512, 256
T = B * S // P
TB = S // P
DC = D // P
QK = D // 8
LOC = D
E, I, K = 32, 128, 4
EW = E + 1
SLOTS = 64
NEG = -1.0e30
EPS = 1e-5
ALPHA = 7.0
LN2 = 0.6931471805599453
AHEAD = 8
RING = 3
SQ_UP = 50
LN_EXP_SET = 6

UP = 64.0
WE = 2 * 2 * I + D

C_ID, C_LT, C_ONE, C_IOTA = 0, P, 2 * P, 3 * P
C_REL, C_MASK = 4 * P, 4 * P + S
C_TOK = C_MASK + S
C_PID = C_TOK + T
C_TRI = C_PID + 1
NCONST = C_TRI + 2 * E

X_Q, X_K = 0, QK
X_LIN, X_PRE, X_VAL = 2 * QK, 2 * QK + LOC, 2 * QK + 2 * LOC
NEXP = 2 * QK + 4 * D


def attn_moe_program(nc, x, consts, small, rbias, expand, project, router, experts, out):
    x1_dram = nc.dram_tensor("x1_rows", [B * S, D], F32)
    y_dram = nc.dram_tensor("slot_rows", [SLOTS * P, D], F32)

    with ExitStack() as ctx:
        def sb(name, shape, dt=F32):
            return ctx.enter_context(nc.sbuf_tensor(name, shape, dt))

        def sem(name):
            return ctx.enter_context(nc.semaphore(name))

        bank = [ctx.enter_context(nc.psum_tensor(f"bank{n}", [P, 512], F32)) for n in range(8)]

        w_hi = sb("w_hi", [P, EW * WE], F16)
        w_lo = sb("w_lo", [P, EW * WE], F16)
        w_in = sb("w_in", [P, RING, WE])
        cst = sb("cst", [P, NCONST])
        sml = sb("sml", [P, 2 * DC + 1])
        bias_e = sb("bias_e", [P, E])
        ex_w = sb("ex_w", [P, DC, NEXP])
        pj_w = sb("pj_w", [P, 2 * DC, D])
        rt_w = sb("rt_w", [P, DC, E])
        x_sb = sb("x_sb", [P, T, D])
        z_sb = sb("z_sb", [P, T, D])
        x1 = z_sb
        hT = sb("hT", [P, DC, B * S])
        x1T = hT
        qT = sb("qT", [QK, B * S])
        kT = sb("kT", [QK, B * S])
        locT = sb("locT", [P, DC, B * S])
        val = sb("val", [P, T, D])
        gl = sb("gl", [P, 2, S])
        gv = sb("gv", [P, 2, D])
        bmat = sb("bmat", [P, S])
        s_sb = gl
        p_sb = sb("p_sb", [P, 2, S])
        pT = sb("pT", [P, S])
        aT = sb("aT", [P, 2, D])
        y1 = gv
        bst = sb("bst", [P, T, 6])
        mv = sb("mv", [P, T, 2])
        rs = sb("rs", [P, T])
        nt = sb("nt", [P, T, 2])
        mxs = sb("mxs", [P, T, 4])
        pb = sb("pb", [P, 8])
        sc16 = sb("sc16", [P, 4 * P], F16)
        lg = sb("lg", [P, T, E])
        ra = sb("ra", [P, T, E])
        re_ = sb("re_", [P, T, E])
        rb = sb("rb", [P, T, E])
        rc = sb("rc", [P, T, E])
        score = sb("score", [P, T, E])
        sel = sb("sel", [P, T, E])
        top = sb("top", [P, T, 8])
        topi = sb("topi", [P, T, 8], U32)
        topf = sb("topf", [P, T, K], F16)
        oh = sb("oh", [P, T, K, E], F16)
        prod = cst[:, C_REL:C_REL + T * K * E].rearrange("p (t k e) -> p t k e", t=T, k=K)
        pk = sb("pk", [P, T, K])
        psum_k = sb("psum_k", [P, T, 2])
        ntile_i = sb("ntile_i", [P, E], I32)
        ntile_j = sb("ntile_j", [P, E], I32)
        ntile = sb("ntile", [P, E])
        ntd = sb("ntd", [E, E])
        ntcol = sb("ntcol", [E, 1])
        base = sb("base", [P, E])
        ends = sb("ends", [P, E])
        posb = sb("posb", [P, T, E])
        slot_f = sb("slot_f", [P, T * K])
        slot_i = sb("slot_i", [P, T * K], I32)
        slot_t = sb("slot_t", [P, 2, T * K], I32)
        slot_r = sb("slot_r", [P, 2, T * K], F16)
        te_col = sb("te_col", [P, 1])
        te_row = sb("te_row", [1, SLOTS], I32)
        token = sb("token", [P, SLOTS], I32)
        ohr = ex_w[:, :, :].rearrange("p c n -> p (c n)")[:, 0:T * K * P // 2].bitcast(F16).rearrange("p (r n) -> p r n", n=T * K)
        idt = gl[:, :, :].rearrange("p a n -> p (a n)").bitcast(F16).rearrange("p (s n) -> p s n", n=T * K)
        xg = val
        y_sb = hT[:, 0, :].rearrange("p (a n) -> p a n", a=4)
        work = x_sb[:, :, :].rearrange("p t d -> p (t d)")

        def pair(at, width, dt=F32):
            both = work[:, at:at + 2 * width]
            return (both if dt == F32 else both.bitcast(dt)).rearrange("p (a n) -> p a n", a=2)

        xT, gu = pair(0, D, F16), pair(2 * D, 2 * I)
        sg, hh, hTs = pair(4 * D, I), pair(4 * D + 2 * I, I), pair(4 * D + 4 * I, P, F16)
        shared = locT[:, :, :].rearrange("p c (t d) -> p (c t) d", d=D)
        yg = w_hi[:, 0:2 * T * K * D].bitcast(F32).rearrange("p (j d) -> p j d", d=D)
        acc = s_sb[:, :, 0:D]
        fin = p_sb[:, :, 0:D]

        ident = cst[:, C_ID:C_ID + P]
        before16 = sc16[:, P:2 * P]
        ones16 = sc16[:, 2 * P:3 * P]
        iota16 = sc16[:, 3 * P:4 * P]

        ld_x = [sem(f"ld_x{b}") for b in range(B)]
        ld_c = sem("ld_c")
        ld_s = sem("ld_s")
        ld_id = sem("ld_id")
        ld_b = sem("ld_b")
        ld_ex = sem("ld_ex")
        ld_val = sem("ld_val")
        ld_pj = sem("ld_pj")
        ld_w = [sem(f"ld_w{n}") for n in range(RING)]
        whi_ready = sem("whi_ready")
        wlo_ready = sem("wlo_ready")
        vec = sem("vec")
        act_ = sem("act_")
        consts_ready = sem("consts_ready")
        var_ready = sem("var_ready")
        rstd_ready = sem("rstd_ready")
        z_ready = sem("z_ready")
        zt_done = sem("zt_done")
        h_ready = sem("h_ready")
        ex_done = sem("ex_done")
        qk_ready = sem("qk_ready")
        gelu_ready = sem("gelu_ready")
        geglu_ready = sem("geglu_ready")
        pos_ready = sem("pos_ready")
        sc_done = sem("sc_done")
        smax_ready = sem("smax_ready")
        exp_ready = sem("exp_ready")
        p_ready = sem("p_ready")
        pt_done = sem("pt_done")
        pt_ready = sem("pt_ready")
        av_done = sem("av_done")
        at_ready = sem("at_ready")
        pj_done = sem("pj_done")
        y1_ready = sem("y1_ready")
        rstd2_ready = sem("rstd2_ready")
        x1_ready = sem("x1_ready")
        x1t_done = sem("x1t_done")
        x1t_ready = sem("x1t_ready")
        lg_done = sem("lg_done")
        x1_stored = sem("x1_stored")
        r_dve = sem("r_dve")
        r_act = sem("r_act")
        oh_ready = sem("oh_ready")
        pos_done = sem("pos_done")
        ntcol_ready = sem("ntcol_ready")
        start_done = sem("start_done")
        te_ready = sem("te_ready")
        ter_done = sem("ter_done")
        te_loaded = sem("te_loaded")
        slotr_ready = sem("slotr_ready")
        counted = sem("counted")
        tile1h_ready = sem("tile1h_ready")
        idt_ready = sem("idt_ready")
        ohr_ready = sem("ohr_ready")
        list_done = sem("list_done")
        token_ready = sem("token_ready")
        slots_ready = sem("slots_ready")
        gath = [sem(f"gath{n}") for n in range(AHEAD)]
        xt_done = sem("xt_done")
        xth_ready = sem("xth_ready")
        xt_ready = sem("xt_ready")
        gu_done = sem("gu_done")
        clipped = sem("clipped")
        silu_ready = sem("silu_ready")
        hh_ready = sem("hh_ready")
        ht_done = sem("ht_done")
        hth_ready = sem("hth_ready")
        ht_ready = sem("ht_ready")
        dn_done = sem("dn_done")
        y_ready = sem("y_ready")
        y_stored = [sem(f"y_stored{n}") for n in range(4)]
        yg_in = [sem(f"yg_in{t}") for t in range(T)]
        var3_ready = sem("var3_ready")
        rstd3_ready = sem("rstd3_ready")
        fin_ready = sem("fin_ready")
        out_stored = [sem(f"out_stored{n}") for n in range(2)]

        block = ctx.enter_context(nc.Block())

        JOBS = 6 + TB

        def released(n):
            b, j = divmod(n, JOBS)
            if j < 2:
                return qk_ready, 2 * b + j + 1
            if j in (2, 4):
                return gelu_ready, 6 * b + j // 2
            return geglu_ready, 6 * b + (j // 2 if j < 6 else j - 3)

        x_rows = x.rearrange("b (t p) d -> p (b t) d", p=P)
        out_rows = out.rearrange("b (t p) d -> p (b t) d", p=P)
        x1_rows = x1_dram.ap().rearrange("(t p) d -> t p d", p=P)
        y_rows = y_dram.ap()
        ST = SLOTS + T

        LAG_PT, LAG_AV, LAG_PJ, LAG_FIN, LAG_XT, LAG_LG = 1, 2, 3, 4, 5, 6

        @block.sync
        def _(sp):
            sp.dma_start(x_sb[:, 0:TB, :], x_rows[:, 0:TB, :]).then_inc(ld_x[0], 16)
            sp.dma_start(cst[:, 0:P], consts[:, 0:P]).then_inc(ld_id, 16)
            sp.dma_start(sml[:, :], small).then_inc(ld_s, 16)
            sp.dma_start(ex_w[:, :, 0:X_VAL], expand[:, :, 0:X_VAL]).then_inc(ld_ex, 16)
            sp.dma_start(x_sb[:, TB:T, :], x_rows[:, TB:T, :]).then_inc(ld_x[1], 16)
            sp.dma_start(ex_w[:, :, X_VAL:NEXP], expand[:, :, X_VAL:NEXP]).then_inc(ld_val, 16)
            sp.dma_start(cst[:, P:NCONST], consts[:, P:NCONST]).then_inc(ld_c, 16)
            sp.dma_start(bias_e[:, :], rbias.to_broadcast([P, E])).then_inc(ld_b, 16)
            sp.dma_start(pj_w[:, :, :], project).then_inc(ld_pj, 16)
            sp.dma_start(rt_w[:, :, :], router).then_inc(ld_pj, 16)
            for e in range(RING):
                sp.dma_start(w_in[:, e, :], experts[:, e, :]).then_inc(ld_w[e], 16)
            with sp.Fori(1, EW // RING) as n:
                for j in range(RING):
                    sp.wait_ge(wlo_ready, RING * n + (j - RING + 1))
                    sp.dma_start(w_in[:, j, :], experts[:, bass.ds(RING * n + j, 1), :].rearrange("p o w -> p (o w)")).then_inc(ld_w[j], 16)

            for t in range(T):
                sp.wait_ge(x1_ready, t + 1)
                sp.dma_start(x1_rows[t], x1[:, t, :]).then_inc(x1_stored, 16)

            with sp.Fori(0, SLOTS // 4) as n:
                for j in range(4):
                    sp.wait_ge(y_ready, 4 * n + (j + 1))
                    sp.dma_start(y_rows[bass.ds(n * (4 * P) + j * P, P), :], y_sb[:, j, :]).then_inc(y_stored[j], 16)
            for t in range(T):
                sp.wait_ge(fin_ready, t + 1)
                sp.dma_start(out_rows[:, t, :], fin[:, t % 2, :]).then_inc(out_stored[t % 2], 16)
            for n in range(2):
                sp.wait_ge(out_stored[n], 16 * T // 2)

        @block.gpsimd
        def _(pool):
            pool.wait_ge(consts_ready, 1)
            pool.wait_ge(ex_done, 2 * JOBS)
            pool.tensor_copy(ohr[:, :, :], iota16.unsqueeze(2).to_broadcast([P, P, T * K])).then_inc(counted, 1)
            pool.wait_ge(exp_ready, T)
            pool.tensor_copy(idt[:, :, :], iota16[:, 0:SLOTS].unsqueeze(2).to_broadcast([P, SLOTS, T * K])).then_inc(counted, 1)
            pool.wait_ge(x1_stored, 16 * T)
            pool.wait_ge(token_ready, 1)

            for m in range(SLOTS):
                if m >= AHEAD:
                    pool.wait_ge(xt_done, m - AHEAD + 1)
                pool.indirect_dma_start(
                    xg[:, m % AHEAD, :], None, x1_dram.ap(),
                    bass.IndirectOffsetOnAxis(ap=token[:, m:m + 1], axis=0)).then_inc(gath[m % AHEAD], 16)
            pool.wait_ge(slots_ready, 1)
            for j in range(4):
                pool.wait_ge(y_stored[j], 16 * SLOTS // 4)
            for t in range(T):
                for k in range(K):
                    n = t * K + k
                    pool.indirect_dma_start(
                        yg[:, n, :], None, y_rows,
                        bass.IndirectOffsetOnAxis(ap=slot_i[:, n:n + 1], axis=0)).then_inc(yg_in[t], 16)

        @block.tensor
        def _(pe):
            def turn_z(b):
                for c in range(DC):
                    for i in range(TB):
                        t = b * TB + i
                        pe.wait_ge(z_ready, t + 1)
                        mm = pe.transpose(bank[2 * b + c][:, i * P:(i + 1) * P],
                                          z_sb[:, t, c * P:(c + 1) * P], ident)
                    mm.then_inc(zt_done, 1)

            def expand_mm(n, rows, parts, lhs, rhs):
                if n >= 4:
                    pe.wait_ge(*released(n - 4))
                for c in range(DC):
                    mm = pe.matmul(bank[4 + n % 4][0:parts, 0:rows], lhs(c), rhs(c),
                                   start=(c == 0), stop=(c == DC - 1))
                mm.then_inc(ex_done, 1)

            pe.wait_ge(ld_id, 16)
            turn_z(0)
            for b in range(B):
                pe.wait_ge(h_ready, DC * (b + 1))
                pe.wait_ge(ld_ex, 16)
                toks = slice(b * S, (b + 1) * S)
                n = b * JOBS
                for j, (at, width) in enumerate([(X_Q, QK), (X_K, QK), (X_PRE, P), (X_LIN, P),
                                                 (X_PRE + P, P), (X_LIN + P, P)]):
                    expand_mm(n + j, S, width, lambda c: ex_w[:, c, at:at + width], lambda c: hT[:, c, toks])
                if b == 0:
                    turn_z(1)
                pe.wait_ge(ld_val, 16)
                for i in range(TB):
                    t = b * TB + i
                    expand_mm(n + 6 + i, 2 * D, P, lambda c: hT[:, c, t * P:(t + 1) * P],
                              lambda c: ex_w[:, c, X_VAL:X_VAL + 2 * D])

            def scores(t):
                b, i = divmod(t, TB)
                pe.wait_ge(qk_ready, 2 * (b + 1))
                if t >= 2:
                    pe.wait_ge(smax_ready, t - 1)
                pe.matmul(bank[t % 2][:, 0:(i + 1) * P], qT[:, t * P:(t + 1) * P],
                          kT[:, b * S:b * S + (i + 1) * P], start=True, stop=True).then_inc(sc_done, 1)

            def turn_probs(t):
                pe.wait_ge(p_ready, t + 1)
                if t >= 1:
                    pe.wait_ge(pt_ready, t)
                for j in range(t % TB + 1):
                    mm = pe.transpose(bank[2][:, j * P:(j + 1) * P], p_sb[:, t % 2, j * P:(j + 1) * P], ident)
                mm.then_inc(pt_done, 1)

            def attend(t):
                b, i = divmod(t, TB)
                pe.wait_ge(pt_ready, t + 1)
                pe.wait_ge(geglu_ready, 6 * b + 3 + i)
                if t == 0:
                    pe.wait_ge(*released(2 * JOBS - 4))
                else:
                    pe.wait_ge(at_ready, t)
                for v in range(2):
                    for j in range(i + 1):
                        mm = pe.matmul(bank[4][:, v * P:(v + 1) * P], val[:, b * TB + j, v * P:(v + 1) * P],
                                       pT[:, j * P:(j + 1) * P], start=(j == 0), stop=(j == i))
                mm.then_inc(av_done, 1)

            def project_mm(t):
                pe.wait_ge(at_ready, t + 1)
                pe.wait_ge(ld_pj, 32)
                if t == 0:
                    pe.wait_ge(*released(2 * JOBS - 3))
                else:
                    pe.wait_ge(y1_ready, t)
                for c in range(2 * DC):
                    lhs = locT[:, c, t * P:(t + 1) * P] if c < DC else aT[:, t % 2, (c - DC) * P:(c - DC + 1) * P]
                    mm = pe.matmul(bank[5][:, 0:D], lhs, pj_w[:, c, :], start=(c == 0), stop=(c == 2 * DC - 1))
                mm.then_inc(pj_done, 1)

            def turn_x1(t):
                pe.wait_ge(x1_ready, t + 1)
                if t == 0:
                    pe.wait_ge(*released(2 * JOBS - 2))
                else:
                    pe.wait_ge(x1t_ready, t)
                for c in range(DC):
                    mm = pe.transpose(bank[6][:, c * P:(c + 1) * P], x1[:, t, c * P:(c + 1) * P], ident)
                mm.then_inc(x1t_done, 1)

            def logits(t):
                b, i = divmod(t, TB)
                pe.wait_ge(x1t_ready, t + 1)
                if t == 0:
                    pe.wait_ge(*released(2 * JOBS - 1))
                for c in range(DC):
                    mm = pe.matmul(bank[7 if b else 3][:, i * E:(i + 1) * E], x1T[:, c, t * P:(t + 1) * P],
                                   rt_w[:, c, :], start=(c == 0), stop=(c == DC - 1))
                mm.then_inc(lg_done, 1)

            for s in range(T + LAG_LG):
                for lag, stage in ((0, scores), (LAG_LG, logits), (LAG_XT, turn_x1), (LAG_PJ, project_mm),
                                   (LAG_AV, attend), (LAG_PT, turn_probs)):
                    if 0 <= s - lag < T:
                        stage(s - lag)

            XT, GU, HT, DN = (2, 7), (3, 4), (5, 6), (0, 1)

            def turn_rows(m, j, arrived):
                if isinstance(m, int) and m >= SLOTS:
                    rows = x1[:, m - SLOTS, :]
                else:
                    pe.wait_ge(gath[j % AHEAD], arrived)
                    rows = xg[:, j % AHEAD, :]
                for c in range(DC):
                    mm = pe.transpose(bank[XT[j % 2]][:, c * P:(c + 1) * P], rows[:, c * P:(c + 1) * P], ident)
                mm.then_inc(xt_done, 1)

            def three(dst, xs, ws):
                n = len(xs)
                for c in range(n):
                    for a_, b_ in ((0, 0), (0, 1), (1, 0)):
                        mm = pe.matmul(dst, xs[c][a_], ws[c][b_], start=(c == 0 and a_ + b_ == 0),
                                       stop=(c == n - 1 and a_ == 1))
                return mm

            def gate_up_mm(m, j, w):
                pe.wait_ge(xt_ready, m + 1)
                xs = [[xT[:, j % 2, (part * DC + c) * P:(part * DC + c + 1) * P] for part in range(2)] for c in range(DC)]
                three(bank[GU[j % 2]][:, 0:2 * I], xs, w[0:DC]).then_inc(gu_done, 1)

            def turn_h(m, j):
                pe.wait_ge(hh_ready, m + 1)
                pe.transpose(bank[HT[j % 2]][:, 0:P], hh[:, j % 2, :], ident).then_inc(ht_done, 1)

            def down_mm(m, j, w):
                pe.wait_ge(ht_ready, m + 1)
                three(bank[DN[j % 2]][:, 0:D], [[hTs[:, j % 2, part * P:(part + 1) * P] for part in range(2)]],
                      w[DC:DC + 1]).then_inc(dn_done, 1)

            def rank_mm(half):
                pe.wait_ge(oh_ready, half + 1)
                if half == 0:
                    pe.wait_ge(smax_ready, T - 1)
                for t in range(half * TB, (half + 1) * TB):
                    for k in range(K):
                        first = t == 0 and k == 0
                        n = T - t
                        rhs = oh[:, t, k, :].unsqueeze(1).to_broadcast([P, n, E])
                        pe.matmul(bank[0][:, (t + 1) * E:(T + 1) * E], ones16, rhs,
                                  start=first, stop=False, skip_group_check=True)
                        mm = pe.matmul(bank[0][:, t * E:(t + 1) * E], before16, oh[:, t, k, :],
                                       start=False, stop=(t == T - 1 and k == K - 1), skip_group_check=True)
                if half == 1:
                    mm.then_inc(pos_done, 1)

            def starts_mm():
                pe.wait_ge(ntcol_ready, 1)
                pe.wait_ge(smax_ready, T)
                pe.matmul(bank[1][:, 0:2 * E], ntcol[:, :].to_broadcast([E, P]), cst[0:E, C_TRI:C_TRI + 2 * E],
                          start=True, stop=True).then_inc(start_done, 1)

            def tile_experts_mm():
                pe.wait_ge(te_ready, 1)
                pe.matmul(bank[1][0:1, 0:P], te_col[:, :], ident, start=True, stop=True).then_inc(ter_done, 1)

            def token_list_mm():
                pe.wait_ge(ohr_ready, 1)
                for n in range(T * K):
                    if n % K == 0:
                        pe.wait_ge(idt_ready, n // K + 1)
                    mm = pe.matmul(bank[0][:, 0:SLOTS], ohr[:, :, n], idt[:, :, n],
                                   start=(n == 0), stop=(n == T * K - 1))
                mm.then_inc(list_done, 1)

            rank_mm(0)
            rank_mm(1)
            starts_mm()
            tile_experts_mm()
            token_list_mm()
            pe.wait_ge(te_loaded, 1)
            pe.wait_ge(wlo_ready, EW)
            pe.wait_ge(at_ready, T)
            pe.wait_ge(r_dve, 6)
            pe.wait_ge(token_ready, 1)

            def parts_at(e):
                return [[w[:, bass.ds(e + c * 2 * I, D)] for w in (w_hi, w_lo)] for c in range(DC + 1)]

            def weights_of(first, m, back, count):
                _, es = nc.values_load_multi_w_load_instructions(
                    te_row[0:1, bass.ds(m - back, back + count)], engines=[mybir.EngineType.PE],
                    min_val=0, max_val=(E - 1) * WE,
                    skip_runtime_bounds_check_because="the experts' numbers were bounded where they were counted")
                return {first - back + i: parts_at(e) for i, e in enumerate(es)}

            def step(m, j, weights, arrived):
                whole = not isinstance(m, int)
                if whole or m + 1 < ST:
                    turn_rows(m + 1, j + 1, arrived[(j + 1) // AHEAD])
                if whole or 2 <= m < ST + 2:
                    turn_h(m - 2, j + 2)
                if whole or m < ST:
                    gate_up_mm(m, j, weights[j])
                if whole or m >= 3:
                    down_mm(m - 3, j + 1, weights[j - 3])

            turn_rows(0, 0, 16)
            ws = weights_of(0, 0, 0, AHEAD)
            for m in range(AHEAD):
                step(m, m, ws, [16, 32])
            with pe.Fori(1, SLOTS // AHEAD - 1) as n:
                ws = weights_of(0, AHEAD * n, 4, AHEAD)
                arrived = [pe.snap(16 * n + 16), pe.snap(16 * n + 32)]
                for j in range(AHEAD):
                    step(AHEAD * n + j, j, ws, arrived)
            ws = weights_of(SLOTS - AHEAD, SLOTS - AHEAD, 4, AHEAD)
            for m in range(SLOTS, ST):
                ws[m] = parts_at(E * WE)
            for m in range(SLOTS - AHEAD, ST + 3):
                step(m, m, ws, {(m + 1) // AHEAD: 16 * SLOTS // AHEAD})

        @block.vector
        def _(dve):
            steps = [0]

            def link(ins):
                steps[0] += 1
                ins.then_inc(vec, 1)
                dve.wait_ge(vec, steps[0])

            def polish(cols):
                v, r, a, c = mv[:, cols, 1:2], rs[:, cols].unsqueeze(2), nt[:, cols, 0:1], nt[:, cols, 1:2]
                link(dve.scalar_tensor_tensor(out=a, in0=v, scalar=EPS, in1=r, op0=ALU.add, op1=ALU.mult))
                link(dve.scalar_tensor_tensor(out=c, in0=a, scalar=-0.5, in1=r, op0=ALU.mult, op1=ALU.mult))
                link(dve.scalar_tensor_tensor(out=r, in0=c, scalar=1.5, in1=r, op0=ALU.add, op1=ALU.mult))

            def split_lo(e):
                dve.wait_ge(whi_ready, e + 1)
                cols = slice(e * WE, (e + 1) * WE)
                dve.scalar_tensor_tensor(out=w_lo[:, cols], in0=w_in[:, e % RING, :], scalar=UP, in1=w_hi[:, cols],
                                         op0=ALU.mult, op1=ALU.subtract).then_inc(wlo_ready, 1)

            for b in range(B):
                dve.wait_ge(ld_x[b], 16)
                for t in range(b * TB, (b + 1) * TB):
                    ins = dve.bn_stats(bst[:, t, :], x_sb[:, t, :])
                link(ins)
                for t in range(b * TB, (b + 1) * TB):
                    ins = dve.bn_aggr(mv[:, t, :], bst[:, t, :])
                ins.then_inc(var_ready, 1)
                dve.wait_ge(rstd_ready, b + 1)
                dve.wait_ge(var_ready, b + 1)
                polish(slice(b * TB, (b + 1) * TB))
                for t in range(b * TB, (b + 1) * TB):
                    dve.tensor_scalar(z_sb[:, t, :], x_sb[:, t, :], mv[:, t, 0:1], rs[:, t:t + 1],
                                      ALU.subtract, ALU.mult).then_inc(z_ready, 1)
            dve.wait_ge(ld_id, 16)
            dve.wait_ge(ld_c, 16)
            dve.tensor_copy(sc16[:, :], cst[:, 0:4 * P]).then_inc(consts_ready, 1)
            dve.wait_ge(pos_ready, 1)
            link(dve.scalar_tensor_tensor(out=pb[:, 3:4], in0=sml[:, 2 * DC:2 * DC + 1], scalar=0.0,
                                          in1=pb[:, 2:3], op0=ALU.max, op1=ALU.add))
            link(dve.scalar_tensor_tensor(out=bmat[:, :], in0=cst[:, C_REL:C_REL + S], scalar=pb[:, 3:4],
                                          in1=cst[:, C_MASK:C_MASK + S], op0=ALU.mult, op1=ALU.add))
            experts_left = iter(range(EW))
            for b in range(B):
                for _ in range(2):
                    split_lo(next(experts_left))
                for c in range(2):
                    dve.wait_ge(ex_done, b * JOBS + 4 + 2 * c)
                    dve.wait_ge(gelu_ready, 6 * b + c + 1)
                    dve.tensor_tensor(locT[:, c, b * S:(b + 1) * S], bank[4 + (b * JOBS + 3 + 2 * c) % 4][:, :],
                                      gl[:, c, :], ALU.mult).then_inc(geglu_ready, 1)
                    split_lo(next(experts_left))
                for i in range(TB):
                    dve.wait_ge(gelu_ready, 6 * b + 3 + i)
                    dve.tensor_tensor(val[:, b * TB + i, :], bank[4 + (b * JOBS + 6 + i) % 4][:, 0:D],
                                      gv[:, i % 2, :], ALU.mult).then_inc(geglu_ready, 1)
                    split_lo(next(experts_left))

            def row_max(t):
                i = t % TB
                w = (i + 1) * P
                dve.wait_ge(sc_done, t + 1)
                if t >= 2:
                    dve.wait_ge(exp_ready, t - 1)
                link(dve.tensor_tensor_reduce(s_sb[:, t % 2, 0:w], bank[t % 2][:, 0:w], bmat[:, S - w:S], 1.0,
                                              3.0 * NEG, ALU.add, ALU.max, mxs[:, t, 0:1]))
                dve.tensor_scalar(mxs[:, t, 1:2], mxs[:, t, 0:1], -1.0, None, ALU.mult).then_inc(smax_ready, 1)

            def normalize_probs(t):
                w = (t % TB + 1) * P
                dve.wait_ge(exp_ready, t + 1)
                link(dve.reciprocal(mxs[:, t, 3:4], mxs[:, t, 2:3]))
                dve.tensor_scalar(p_sb[:, t % 2, 0:w], p_sb[:, t % 2, 0:w], mxs[:, t, 3:4], None,
                                  ALU.mult).then_inc(p_ready, 1)

            def residual(t):
                dve.wait_ge(pj_done, t + 1)
                if t >= 2:
                    dve.wait_ge(x1_ready, t - 1)
                link(dve.scalar_tensor_tensor(out=y1[:, t % 2, :], in0=x_sb[:, t, :], scalar=2.0,
                                              in1=bank[5][:, 0:D], op0=ALU.mult, op1=ALU.add))
                link(dve.bn_stats(bst[:, t, :], y1[:, t % 2, :]))
                dve.bn_aggr(mv[:, t, :], bst[:, t, :]).then_inc(y1_ready, 1)

            def finish_x1(t):
                dve.wait_ge(rstd2_ready, t + 1)
                polish(slice(t, t + 1))
                dve.wait_ge(zt_done, B * DC)
                dve.tensor_scalar(x1[:, t, :], y1[:, t % 2, :], mv[:, t, 0:1], rs[:, t:t + 1],
                                  ALU.subtract, ALU.mult).then_inc(x1_ready, 1)

            def half(h):
                ts = slice(h * TB, (h + 1) * TB)
                return [b[:, ts, :] for b in (lg, ra, re_, rb, rc, score, sel)]

            def logits_out(h):
                l = half(h)[0]
                dve.wait_ge(lg_done, (h + 1) * TB)
                dve.tensor_copy(l, bank[7 if h else 3][:, 0:TB * E].rearrange("p (t e) -> p t e", e=E)).then_inc(r_dve, 1)

            def one_plus(h):
                l, a, e, u, d, q, c = half(h)
                dve.wait_ge(r_act, 3 * h + 1)
                dve.tensor_scalar(u, e, 1.0, None, ALU.add).then_inc(r_dve, 1)
                dve.wait_ge(r_dve, 3 * h + 2)
                link(dve.scalar_tensor_tensor(out=d, in0=u, scalar=-1.0, in1=e, op0=ALU.add, op1=ALU.subtract))

            def softplus(h):
                l, a, e, u, d, q, c = half(h)
                dve.wait_ge(r_act, 3 * h + 2)
                link(dve.scalar_tensor_tensor(out=a, in0=l, scalar=0.0, in1=a, op0=ALU.max, op1=ALU.add))
                link(dve.tensor_tensor(a, a, d, ALU.subtract))
                dve.tensor_scalar(a, a, 2.0 ** -110, None, ALU.max).then_inc(r_dve, 1)

            def root(h):
                l, a, e, u, d, q, c = half(h)
                dve.wait_ge(r_dve, 3 * h + 3)
                dve.wait_ge(r_act, 3 * h + 3)
                link(dve.tensor_tensor(e, a, u, ALU.mult))
                link(dve.scalar_tensor_tensor(out=d, in0=e, scalar=-0.5, in1=u, op0=ALU.mult, op1=ALU.mult))
                link(dve.scalar_tensor_tensor(out=q, in0=d, scalar=1.5, in1=e, op0=ALU.add, op1=ALU.mult))

            def greatest(h):
                l, a, e, u, d, q, c = half(h)
                link(dve.tensor_tensor(c, q, bias_e[:, :].unsqueeze(1).to_broadcast([P, TB, E]), ALU.add))
                for t in range(h * TB, (h + 1) * TB):
                    ins = dve.max(top[:, t, :], sel[:, t, :])
                link(ins)

            def one_hots(h):
                ts = slice(h * TB, (h + 1) * TB)
                for t in range(h * TB, (h + 1) * TB):
                    ins = dve.max_index(topi[:, t, :], top[:, t, :], sel[:, t, :])
                link(ins)
                link(dve.tensor_copy(topf[:, ts, :], topi[:, ts, 0:K]))
                dve.tensor_tensor(oh[:, ts, :, :],
                                  iota16[:, 0:E].unsqueeze(1).unsqueeze(1).to_broadcast([P, TB, K, E]),
                                  topf[:, ts, :].unsqueeze(3).to_broadcast([P, TB, K, E]),
                                  ALU.is_equal).then_inc(oh_ready, 1)

            def chosen_scores(h):
                ts = slice(h * TB, (h + 1) * TB)
                dve.wait_ge(oh_ready, h + 1)
                link(dve.tensor_tensor(prod[:, ts, :, :], oh[:, ts, :, :],
                                       score[:, ts, :].unsqueeze(2).to_broadcast([P, TB, K, E]), ALU.mult))
                link(dve.tensor_reduce(pk[:, ts, :], prod[:, ts, :, :], AX, ALU.add))

            def shares():
                link(dve.tensor_reduce(psum_k[:, :, 0:1], pk[:, :, :], AX, ALU.add))
                link(dve.tensor_scalar(psum_k[:, :, 0:1], psum_k[:, :, 0:1], 1e-20, None, ALU.add))
                link(dve.reciprocal(psum_k[:, :, 1:2], psum_k[:, :, 0:1]))
                link(dve.tensor_tensor(pk[:, :, :], pk[:, :, :], psum_k[:, :, 1:2].to_broadcast([P, T, K]), ALU.mult))

            def count_tiles():
                dve.wait_ge(pos_done, 1)
                link(dve.tensor_scalar(ntile_i[:, :], bank[0][:, T * E:(T + 1) * E], float(P - 1), None, ALU.add))
                link(dve.tensor_scalar(ntile_j[:, :], ntile_i[:, :], 7, None, ALU.logical_shift_right))
                link(dve.tensor_copy(ntile[:, :], ntile_j[:, :]))
                dve.tensor_tensor_reduce(ntd[:, :], ntile[0:E, :], ident[0:E, 0:E], 1.0, 0.0, ALU.mult, ALU.add,
                                         ntcol[:, :]).then_inc(ntcol_ready, 1)

            def tile_experts():
                dve.wait_ge(start_done, 1)
                dve.tensor_scalar(base[:, :], bank[1][:, 0:E], float(P), None, ALU.mult)
                link(dve.tensor_copy(ends[:, :], bank[1][:, E:2 * E]))
                link(dve.tensor_scalar(ends[:, :], ends[:, :], cst[:, C_PID:C_PID + 1], None, ALU.is_le, ALU.add,
                                       accum_out=te_col[:, :]))
                dve.tensor_scalar(te_col[:, :], te_col[:, :], float(E - 1), None, ALU.min).then_inc(te_ready, 1)

            def find_slots():
                link(dve.tensor_tensor(posb[:, :, :], bank[0][:, 0:T * E].rearrange("p (t e) -> p t e", e=E),
                                       base[:, :].unsqueeze(1).to_broadcast([P, T, E]), ALU.add))
                link(dve.tensor_tensor(prod[:, :, :, :], oh[:, :, :, :],
                                       posb[:, :, :].unsqueeze(2).to_broadcast([P, T, K, E]), ALU.mult))
                link(dve.tensor_reduce(slot_f[:, :].rearrange("p (t k) -> p t k", k=K), prod[:, :, :, :], AX, ALU.add))
                link(dve.tensor_copy(slot_i[:, :], slot_f[:, :]))
                dve.tensor_scalar(slot_t[:, 0, :], slot_i[:, :], 7, None, ALU.logical_shift_right)
                link(dve.tensor_scalar(slot_t[:, 1, :], slot_i[:, :], P - 1, None, ALU.bitwise_and))
                dve.tensor_copy(slot_r[:, :, :], slot_t[:, :, :]).then_inc(slotr_ready, 1)
                dve.wait_ge(slotr_ready, 1)

            def expert_rows():
                dve.wait_ge(ter_done, 1)
                dve.tensor_scalar(te_row[:, :], bank[1][0:1, 0:SLOTS], float(WE), None, ALU.mult).then_inc(te_loaded, 1)

            def list_operands():
                dve.wait_ge(counted, 2)
                dve.tensor_tensor(idt[:, :, :], idt[:, :, :],
                                  slot_r[:, 0, :].unsqueeze(1).to_broadcast([P, SLOTS, T * K]), ALU.is_equal).then_inc(tile1h_ready, 1)
                dve.tensor_tensor(ohr[:, :, :], ohr[:, :, :],
                                  slot_r[:, 1, :].unsqueeze(1).to_broadcast([P, P, T * K]), ALU.is_equal).then_inc(ohr_ready, 1)

            def token_list():
                dve.wait_ge(list_done, 1)
                dve.tensor_copy(token[:, :], bank[0][:, 0:SLOTS]).then_inc(token_ready, 1)

            def low_xT(m, j):
                dve.wait_ge(xth_ready, m + 1)
                dve.tensor_tensor(xT[:, j % 2, D:2 * D], bank[(2, 7)[j % 2]][:, 0:D], xT[:, j % 2, 0:D],
                                  ALU.subtract).then_inc(xt_ready, 1)

            def clip(m, j):
                dve.wait_ge(gu_done, m + 1)
                dve.tensor_scalar(gu[:, j % 2, :], bank[(3, 4)[j % 2]][:, 0:2 * I], ALPHA * UP, -ALPHA * UP,
                                  ALU.min, ALU.max).then_inc(clipped, 1)

            def low_hT(m, j):
                dve.wait_ge(hth_ready, m + 1)
                dve.tensor_tensor(hTs[:, j % 2, P:2 * P], bank[(5, 6)[j % 2]][:, 0:P], hTs[:, j % 2, 0:P],
                                  ALU.subtract).then_inc(ht_ready, 1)

            def gate_times_up(m, j):
                dve.wait_ge(silu_ready, m + 1)
                dve.tensor_tensor(hh[:, j % 2, :], sg[:, j % 2, :], gu[:, j % 2, I:2 * I], ALU.mult).then_inc(hh_ready, 1)

            for s in range(T + LAG_LG):
                if 0 <= s - LAG_FIN < T:
                    finish_x1(s - LAG_FIN)
                if s == TB + LAG_LG:
                    one_plus(0)
                for e in islice(experts_left, int(s >= 2)):
                    split_lo(e)
                if 0 <= s - 1 < T:
                    normalize_probs(s - 1)
                if 0 <= s - LAG_PJ < T:
                    residual(s - LAG_PJ)
                if s < T:
                    row_max(s)
                for e in islice(experts_left, int(s >= 1)):
                    split_lo(e)
                if s == TB + LAG_LG - 1:
                    logits_out(0)
                if s == TB + LAG_LG:
                    softplus(0)
                if s == TB + LAG_LG + 1:
                    root(0)
            dve.wait_ge(consts_ready, 1)
            dve.wait_ge(ld_b, 16)
            greatest(0)
            logits_out(1)
            one_hots(0)
            one_plus(1)
            softplus(1)
            root(1)
            greatest(1)
            one_hots(1)
            chosen_scores(1)

            count_tiles()
            tile_experts()
            find_slots()
            expert_rows()
            list_operands()
            token_list()
            chosen_scores(0)
            shares()
            dve.drain().then_inc(slots_ready, 1)

            def step(m, j):
                whole = not isinstance(m, int)
                if whole or m + 1 < ST:
                    low_xT(m + 1, j + 1)
                if whole or 1 <= m < ST + 1:
                    gate_times_up(m - 1, j + 1)
                if whole or m < ST:
                    clip(m, j)
                if whole or 2 <= m:
                    low_hT(m - 2, j)

            low_xT(0, 0)
            step(0, 0)
            step(1, 1)
            with dve.Fori(1, ST // 2 - 1) as n:
                for j in range(2):
                    step(2 * n + j, j)
            for m in range(ST - 2, ST + 2):
                step(m, m)

            def combine(t):
                dve.wait_ge(yg_in[t], 16 * K)
                if t >= 2:
                    dve.wait_ge(fin_ready, t - 1)
                a = acc[:, t % 2, :]
                link(dve.scalar_tensor_tensor(out=a, in0=yg[:, t * K, :], scalar=pk[:, t, 0:1], in1=shared[:, t, :],
                                              op0=ALU.mult, op1=ALU.add))
                for k in range(1, K):
                    link(dve.scalar_tensor_tensor(out=a, in0=yg[:, t * K + k, :], scalar=pk[:, t, k:k + 1], in1=a,
                                                  op0=ALU.mult, op1=ALU.add))
                link(dve.tensor_tensor(a, a, x1[:, t, :], ALU.add))
                link(dve.bn_stats(bst[:, t, :], a))
                dve.bn_aggr(mv[:, t, :], bst[:, t, :]).then_inc(var3_ready, 1)

            def finish(t):
                dve.wait_ge(var3_ready, t + 1)
                dve.wait_ge(rstd3_ready, t + 1)
                polish(slice(t, t + 1))
                if t >= 2:
                    dve.wait_ge(out_stored[t % 2], 16 * (t // 2))
                dve.tensor_scalar(fin[:, t % 2, :], acc[:, t % 2, :], mv[:, t, 0:1], rs[:, t:t + 1],
                                  ALU.subtract, ALU.mult).then_inc(fin_ready, 1)

            for t in range(T + 1):
                if t < T:
                    combine(t)
                if t >= 1:
                    finish(t - 1)

        @block.scalar
        def _(act):
            steps = [0]

            def link(ins):
                steps[0] += 1
                ins.then_inc(act_, 1)
                act.wait_ge(act_, steps[0])

            def rstd(cols, ready):
                r = rs[:, cols].unsqueeze(2)
                act.activation(r, mv[:, cols, 1:2], ACT.Ln, bias=EPS).then_inc(act_, 1)
                steps[0] += 1
                act.wait_ge(act_, steps[0])
                act.activation(r, r, ACT.Exp, scale=-0.5).then_inc(ready, 1)

            def load_ln_exp():
                act.add_instruction(mybir.InstLoadActFuncSet(
                    act_func_set_id=LN_EXP_SET, name=nc.get_next_instruction_name(), engine=mybir.EngineType.Activation))

            def split_hi(e):
                act.wait_ge(ld_w[e % RING], 16 * (e // RING + 1))
                act.activation(w_hi[:, e * WE:(e + 1) * WE], w_in[:, e % RING, :], ACT.Copy, scale=UP).then_inc(whi_ready, 1)

            def copy_hT(b):
                for c in range(DC):
                    act.wait_ge(zt_done, b * DC + c + 1)
                    act.activation(hT[:, c, b * S:(b + 1) * S], bank[2 * b + c][:, :], ACT.Identity,
                                   bias=sml[:, DC + c:DC + c + 1], scale=sml[:, c:c + 1]).then_inc(h_ready, 1)

            load_ln_exp()
            act.wait_ge(var_ready, 1)
            rstd(slice(0, TB), rstd_ready)
            act.wait_ge(ld_s, 16)
            link(act.activation(pb[:, 0:1], sml[:, 2 * DC:2 * DC + 1], ACT.Abs))
            link(act.activation(pb[:, 1:2], pb[:, 0:1], ACT.Exp, scale=-1.0))
            act.activation(pb[:, 2:3], pb[:, 1:2], ACT.Ln, bias=1.0).then_inc(pos_ready, 1)
            copy_hT(0)
            act.wait_ge(var_ready, 2)
            rstd(slice(TB, T), rstd_ready)
            experts_left = iter(range(EW))
            for b in range(B):
                n = b * JOBS
                cols = slice(b * S, (b + 1) * S)
                act.wait_ge(ex_done, n + 1)
                act.activation(qT[:, cols], bank[4 + n % 4][0:QK, :], ACT.Copy, scale=float(QK) ** -0.5).then_inc(qk_ready, 1)
                split_hi(next(experts_left))
                act.wait_ge(ex_done, n + 2)
                act.activation(kT[:, cols], bank[4 + (n + 1) % 4][0:QK, :], ACT.Copy).then_inc(qk_ready, 1)
                split_hi(next(experts_left))
                for c in range(2):
                    act.wait_ge(ex_done, n + 3 + 2 * c)
                    if b:
                        act.wait_ge(geglu_ready, 6 * (b - 1) + c + 1)
                    act.activation(gl[:, c, :], bank[4 + (n + 2 + 2 * c) % 4][:, :], ACT.Gelu).then_inc(gelu_ready, 1)
                    split_hi(next(experts_left))
                if b == 0:
                    copy_hT(1)
                for i in range(TB):
                    act.wait_ge(ex_done, n + 7 + i)
                    if i >= 2:
                        act.wait_ge(geglu_ready, 6 * b + 3 + i - 2)
                    elif b:
                        act.wait_ge(geglu_ready, 6 * (b - 1) + 3 + TB - 2 + i)
                    act.activation(gv[:, i % 2, :], bank[4 + (n + 6 + i) % 4][:, D:2 * D], ACT.Gelu).then_inc(gelu_ready, 1)
                    split_hi(next(experts_left))

            load_ln_exp()

            def exps(t):
                w = (t % TB + 1) * P
                act.wait_ge(smax_ready, t + 1)
                if t >= 2:
                    act.wait_ge(pt_done, t - 1)
                act.activation(p_sb[:, t % 2, 0:w], s_sb[:, t % 2, 0:w], ACT.Exp, bias=mxs[:, t, 1:2],
                               accum_out=mxs[:, t, 2:3]).then_inc(exp_ready, 1)

            def copy_pT(t):
                w = (t % TB + 1) * P
                act.wait_ge(pt_done, t + 1)
                if t >= 1:
                    act.wait_ge(av_done, t)
                act.activation(pT[:, 0:w], bank[2][:, 0:w], ACT.Copy).then_inc(pt_ready, 1)

            def copy_aT(t):
                act.wait_ge(av_done, t + 1)
                if t >= 2:
                    act.wait_ge(pj_done, t - 1)
                act.activation(aT[:, t % 2, :], bank[4][:, 0:D], ACT.Copy).then_inc(at_ready, 1)

            def rstd2(t):
                act.wait_ge(y1_ready, t + 1)
                rstd(slice(t, t + 1), rstd2_ready)

            def copy_x1T(t):
                act.wait_ge(x1t_done, t + 1)
                act.wait_ge(ex_done, 2 * JOBS)
                act.activation(x1T[:, :, t * P:(t + 1) * P], bank[6][:, 0:D].rearrange("p (c n) -> p c n", c=DC),
                               ACT.Copy).then_inc(x1t_ready, 1)

            def exp_of_logits(h):
                ts = slice(h * TB, (h + 1) * TB)
                act.wait_ge(r_dve, 3 * h + 1)
                link(act.activation(ra[:, ts, :], lg[:, ts, :], ACT.Abs))
                act.activation(re_[:, ts, :], ra[:, ts, :], ACT.Exp, scale=-1.0).then_inc(r_act, 1)

            def ln_of_sum(h):
                ts = slice(h * TB, (h + 1) * TB)
                act.wait_ge(r_dve, 3 * h + 2)
                act.activation(ra[:, ts, :], rb[:, ts, :], ACT.Ln).then_inc(r_act, 1)

            def inverse_root(h):
                ts = slice(h * TB, (h + 1) * TB)
                act.wait_ge(r_dve, 3 * h + 3)
                link(act.activation(rb[:, ts, :], ra[:, ts, :], ACT.Ln, scale=2.0 ** SQ_UP))
                act.activation(rb[:, ts, :], rb[:, ts, :], ACT.Exp, scale=-0.5, bias=0.5 * SQ_UP * LN2).then_inc(r_act, 1)

            for s in range(T + LAG_LG):
                for lag, stage in ((LAG_XT, copy_x1T), (None, split_hi), (LAG_PJ, rstd2), (LAG_AV, copy_aT),
                                   (LAG_PT, copy_pT), (0, exps), (None, split_hi)):
                    if lag is None:
                        for e in islice(experts_left, int(s >= 1)):
                            stage(e)
                    elif 0 <= s - lag < T:
                        stage(s - lag)
                if s == TB + LAG_LG - 1:
                    exp_of_logits(0)
                if s == TB + LAG_LG:
                    ln_of_sum(0)
                if s == TB + LAG_LG + 1:
                    inverse_root(0)
            exp_of_logits(1)
            ln_of_sum(1)
            inverse_root(1)

            act.wait_ge(tile1h_ready, 1)
            for t in range(T):
                part = idt[:, :, t * K:(t + 1) * K]
                act.activation(part, part, ACT.Copy, scale=cst[:, C_TOK + t:C_TOK + t + 1]).then_inc(idt_ready, 1)

            def high_xT(m, j):
                act.wait_ge(xt_done, m + 1)
                act.activation(xT[:, j % 2, 0:D], bank[(2, 7)[j % 2]][:, 0:D], ACT.Copy).then_inc(xth_ready, 1)

            def silu(m, j):
                act.wait_ge(clipped, m + 1)
                act.activation(sg[:, j % 2, :], gu[:, j % 2, 0:I], ACT.Silu, scale=1.0 / UP).then_inc(silu_ready, 1)

            def high_hT(m, j):
                act.wait_ge(ht_done, m + 1)
                act.activation(hTs[:, j % 2, 0:P], bank[(5, 6)[j % 2]][:, 0:P], ACT.Copy).then_inc(hth_ready, 1)

            def copy_y(m, j):
                if isinstance(m, int) and m >= SLOTS:
                    dst = shared[:, m - SLOTS, :]
                else:
                    if not (isinstance(m, int) and m < 4):
                        act.wait_ge(y_stored[j % 4], 16 * (m // 4) if isinstance(m, int) else 4 * m - 4 * (j % 4))
                    dst = y_sb[:, j % 4, :]
                act.wait_ge(dn_done, m + 1)
                act.activation(dst, bank[j % 2][:, 0:D], ACT.Copy, scale=1.0 / (UP * UP)).then_inc(y_ready, 1)

            def step(m, j):
                whole = not isinstance(m, int)
                if whole or m + 1 < ST:
                    high_xT(m + 1, j + 1)
                if whole or 1 <= m < ST + 1:
                    silu(m - 1, j + 1)
                if whole or m >= 4:
                    copy_y(m - 4, j)
                if whole or 2 <= m < ST + 2:
                    high_hT(m - 2, j + 2)

            high_xT(0, 0)
            for m in range(8):
                step(m, m)
            with act.Fori(2, SLOTS // 4) as n:
                for j in range(4):
                    step(4 * n + j, j)
            for m in range(SLOTS, ST + 4):
                step(m, m)
            load_ln_exp()

            for t in range(T):
                act.wait_ge(var3_ready, t + 1)
                rstd(slice(t, t + 1), rstd3_ready)


def _constants(np):
    c = np.zeros((P, NCONST), np.float32)
    p = np.arange(P)[:, None]
    n = np.arange(P)[None, :]
    c[:, C_ID:C_ID + P] = p == n
    c[:, C_LT:C_LT + P] = p < n
    c[:, C_ONE:C_ONE + P] = 1.0
    c[:, C_IOTA:C_IOTA + P] = n
    rel = np.arange(S)[None, :] - (S - P) - p
    c[:, C_REL:C_REL + S] = np.minimum(rel, 0)
    c[:, C_MASK:C_MASK + S] = np.where(rel > 0, NEG, 0.0)
    c[:, C_TOK:C_TOK + T] = np.arange(T)[None, :] * P + p
    c[:, C_PID:C_PID + 1] = p
    e = np.arange(E)[None, :]
    c[:, C_TRI:C_TRI + E] = p < e
    c[:, C_TRI + E:C_TRI + 2 * E] = p <= e
    return c


def kernel(**inputs):
    import numpy as np
    import concourse.bacc as bacc
    from concourse.bass_utils import run_bass_kernel_spmd as run

    a = {k: np.asarray(v) for k, v in inputs.items()}

    def chunked(w, lead):
        return w.T.reshape(lead, P, w.shape[0]).transpose(1, 0, 2)

    ex = a["L0_attn_expand"]
    loc, value = 2 * QK, 2 * QK + LOC
    pre = 2 * QK + 2 * D
    ex = np.concatenate([ex[0:2 * QK], ex[loc:loc + D], ex[pre:pre + D], ex[value:value + D], ex[pre + D:pre + 2 * D]])
    gate = np.concatenate([a["L0_ffn_gate_w"], a["L0_ffn_shared_gate_w"][None]])
    up = np.concatenate([a["L0_ffn_up_w"], a["L0_ffn_shared_up_w"][None]])
    dn = np.concatenate([a["L0_ffn_down_w"], a["L0_ffn_shared_down_w"][None]])
    gu = np.concatenate([gate, up], axis=1)
    gu = gu.transpose(2, 0, 1).reshape(DC, P, EW, 2 * I).transpose(1, 2, 0, 3).reshape(P, EW, 2 * 2 * I)
    small = np.concatenate([a["L0_attn_ln_gamma"].reshape(DC, P).T, a["L0_attn_ln_beta"].reshape(DC, P).T,
                            np.broadcast_to(a["L0_attn_pos_mult"].reshape(1, 1), (P, 1))], axis=1)
    arrays = {
        "x": a["L0_attn_x"],
        "consts": _constants(np),
        "small": small,
        "rbias": a["L0_ffn_expert_bias"].reshape(1, E),
        "expand": chunked(ex, DC),
        "project": chunked(a["L0_attn_project"], 2 * DC),
        "router": chunked(a["L0_ffn_router_w"], DC),
        "experts": np.concatenate([gu, dn.transpose(2, 0, 1)], axis=2),
    }
    arrays = {k: np.ascontiguousarray(v) for k, v in arrays.items()}
    nc = bacc.Bacc("TRN2", target_bir_lowering=False, num_devices=1)
    args = {k: nc.dram_tensor(f"in_{k}", v.shape, mybir.dt.from_np(v.dtype), kind="ExternalInput").ap()
            for k, v in arrays.items()}
    args["out"] = nc.dram_tensor("out_0", (B, S, D), F32, kind="ExternalOutput").ap()
    attn_moe_program(nc, **args)
    r = run(nc, [{f"in_{k}": v for k, v in arrays.items()}], core_ids=[0])
    return r.results[0]["out_0"]
```

```python
from contextlib import ExitStack
from itertools import islice

import concourse.bass as bass
from concourse import mybir

F32 = mybir.dt.float32
F16 = mybir.dt.float16
I32 = mybir.dt.int32
U32 = mybir.dt.uint32
ALU = mybir.AluOpType
ACT = mybir.ActivationFunctionType
AX = mybir.AxisListType.X

P = 128
B, S, D = 2, 512, 256
T = B * S // P
TB = S // P
DC = D // P
QK = D // 8
LOC = D
E, I, K = 32, 128, 4
EW = E + 1
SLOTS = 64
FAR = 1.0e30
EPS = 1e-5
ALPHA = 7.0
LN2 = 0.6931471805599453
AHEAD = 8
RING = 3
SQ_UP = 50
LN_EXP_SET = 6

UP = 64.0
WE = 2 * 2 * I + D

C_ID, C_LT, C_ONE, C_IOTA = 0, P, 2 * P, 3 * P
C_REL, C_MASK = 4 * P, 4 * P + S
C_TOK = C_MASK + S
C_PID = C_TOK + T
C_TRI = C_PID + 1
NCONST = C_TRI + 2 * E

X_Q, X_K = 0, QK
X_LIN, X_PRE, X_VAL = 2 * QK, 2 * QK + LOC, 2 * QK + 2 * LOC
NEXP = 2 * QK + 4 * D


def attn_moe_program(nc, x, consts, small, rbias, expand, project, router, experts, out):
    x1_dram = nc.dram_tensor("x1_rows", [B * S, D], F32)
    y_dram = nc.dram_tensor("slot_rows", [SLOTS * P, D], F32)

    with ExitStack() as ctx:
        def sb(name, shape, dt=F32):
            return ctx.enter_context(nc.sbuf_tensor(name, shape, dt))

        def sem(name):
            return ctx.enter_context(nc.semaphore(name))

        bank = [ctx.enter_context(nc.psum_tensor(f"bank{n}", [P, 512], F32)) for n in range(8)]

        w_hi = sb("w_hi", [P, EW * WE], F16)
        w_lo = sb("w_lo", [P, EW * WE], F16)
        w_in = sb("w_in", [P, RING, WE])
        cst = sb("cst", [P, NCONST])
        sml = sb("sml", [P, 2 * DC + 1])
        bias_e = sb("bias_e", [P, E])
        ex_w = sb("ex_w", [P, DC, NEXP])
        pj_w = sb("pj_w", [P, 2 * DC, D])
        rt_w = sb("rt_w", [P, DC, E])
        x_sb = sb("x_sb", [P, T, D])
        z_sb = sb("z_sb", [P, T, D])
        x1 = z_sb
        hT = sb("hT", [P, DC, B * S])
        x1T = hT
        qT = sb("qT", [QK, B * S])
        kT = sb("kT", [QK, B * S])
        locT = sb("locT", [P, DC, B * S])
        val = sb("val", [P, T, D])
        gl = sb("gl", [P, 2, S])
        gv = sb("gv", [P, 2, D])
        bmat = sb("bmat", [P, S])
        s_sb = gl
        p_sb = sb("p_sb", [P, 2, S])
        pT = sb("pT", [P, S])
        aT = sb("aT", [P, 2, D])
        y1 = gv
        bst = sb("bst", [P, T, 6])
        mv = sb("mv", [P, T, 2])
        rs = sb("rs", [P, T])
        nt = sb("nt", [P, T, 2])
        mxs = sb("mxs", [P, T, 3])
        pb = sb("pb", [P, 8])
        sc16 = sb("sc16", [P, 4 * P], F16)
        lg = sb("lg", [P, T, E])
        ra = sb("ra", [P, T, E])
        re_ = sb("re_", [P, T, E])
        rb = sb("rb", [P, T, E])
        rc = sb("rc", [P, T, E])
        score = sb("score", [P, T, E])
        sel = sb("sel", [P, T, E])
        top = sb("top", [P, T, 8])
        topi = sb("topi", [P, T, 8], U32)
        topf = sb("topf", [P, T, K], F16)
        oh = sb("oh", [P, T, K, E], F16)
        prod = cst[:, C_REL:C_REL + T * K * E].rearrange("p (t k e) -> p t k e", t=T, k=K)
        pk = sb("pk", [P, T, K])
        psum_k = sb("psum_k", [P, T, 2])
        ntile_i = sb("ntile_i", [P, E], I32)
        ntile_j = sb("ntile_j", [P, E], I32)
        ntile = sb("ntile", [P, E])
        ntd = sb("ntd", [E, E])
        ntcol = sb("ntcol", [E, 1])
        base = sb("base", [P, E])
        ends = sb("ends", [P, E])
        posb = sb("posb", [P, T, E])
        slot_f = sb("slot_f", [P, T * K])
        slot_i = sb("slot_i", [P, T * K], I32)
        slot_t = sb("slot_t", [P, 2, T * K], I32)
        slot_r = sb("slot_r", [P, 2, T * K], F16)
        te_col = sb("te_col", [P, 1])
        te_row = sb("te_row", [1, SLOTS], I32)
        token = sb("token", [P, SLOTS], I32)
        ohr = ex_w[:, :, :].rearrange("p c n -> p (c n)")[:, 0:T * K * P // 2].bitcast(F16).rearrange("p (r n) -> p r n", n=T * K)
        idt = gl[:, :, :].rearrange("p a n -> p (a n)").bitcast(F16).rearrange("p (s n) -> p s n", n=T * K)
        xg = val
        y_sb = hT[:, 0, :].rearrange("p (a n) -> p a n", a=4)
        xT = hT[:, 1, :].bitcast(F16).rearrange("p (a n) -> p a n", a=4)
        work = x_sb[:, :, :].rearrange("p t d -> p (t d)")

        def ring(at, count, width):
            return work[:, at:at + count * width].rearrange("p (a n) -> p a n", a=count)

        gu, sg, hh = ring(0, 2, 2 * I), ring(4 * I, 2, I), ring(6 * I, 2, I)
        hTs = work[:, 8 * I:8 * I + 4 * P].bitcast(F16).rearrange("p (a n) -> p a n", a=4)
        shared = locT[:, :, :].rearrange("p c (t d) -> p (c t) d", d=D)
        yg = w_hi[:, 0:2 * T * K * D].bitcast(F32).rearrange("p (j d) -> p j d", d=D)
        acc = s_sb[:, :, 0:D]
        fin = p_sb[:, :, 0:D]

        ident = cst[:, C_ID:C_ID + P]
        before16 = sc16[:, P:2 * P]
        ones16 = sc16[:, 2 * P:3 * P]
        iota16 = sc16[:, 3 * P:4 * P]

        ld_x = [sem(f"ld_x{b}") for b in range(B)]
        ld_c = sem("ld_c")
        ld_s = sem("ld_s")
        ld_id = sem("ld_id")
        ld_b = sem("ld_b")
        ld_ex = sem("ld_ex")
        ld_val = sem("ld_val")
        ld_pj = sem("ld_pj")
        ld_w = [sem(f"ld_w{n}") for n in range(RING)]
        whi_ready = sem("whi_ready")
        wlo_ready = sem("wlo_ready")
        vec = sem("vec")
        act_ = sem("act_")
        consts_ready = sem("consts_ready")
        var_ready = sem("var_ready")
        rstd_ready = sem("rstd_ready")
        z_ready = sem("z_ready")
        zt_done = sem("zt_done")
        h_ready = sem("h_ready")
        ex_done = sem("ex_done")
        qk_ready = sem("qk_ready")
        gelu_ready = sem("gelu_ready")
        geglu_ready = sem("geglu_ready")
        pos_ready = sem("pos_ready")
        sc_done = sem("sc_done")
        smax_ready = sem("smax_ready")
        exp_ready = sem("exp_ready")
        p_ready = sem("p_ready")
        pt_done = sem("pt_done")
        pt_ready = sem("pt_ready")
        av_done = sem("av_done")
        at_ready = sem("at_ready")
        pj_done = sem("pj_done")
        y1_ready = sem("y1_ready")
        rstd2_ready = sem("rstd2_ready")
        x1_ready = sem("x1_ready")
        x1t_done = sem("x1t_done")
        x1t_ready = sem("x1t_ready")
        lg_done = sem("lg_done")
        x1_stored = sem("x1_stored")
        r_dve = sem("r_dve")
        r_act = sem("r_act")
        oh_ready = sem("oh_ready")
        pos_done = sem("pos_done")
        ntcol_ready = sem("ntcol_ready")
        start_done = sem("start_done")
        te_ready = sem("te_ready")
        ter_done = sem("ter_done")
        te_loaded = sem("te_loaded")
        slotr_ready = sem("slotr_ready")
        counted = sem("counted")
        tile1h_ready = sem("tile1h_ready")
        idt_ready = sem("idt_ready")
        ohr_ready = sem("ohr_ready")
        list_done = sem("list_done")
        token_ready = sem("token_ready")
        slots_ready = sem("slots_ready")
        gath = [sem(f"gath{n}") for n in range(AHEAD)]
        xt_done = sem("xt_done")
        xth_ready = sem("xth_ready")
        xt_ready = sem("xt_ready")
        gu_done = sem("gu_done")
        clipped = sem("clipped")
        silu_ready = sem("silu_ready")
        hh_ready = sem("hh_ready")
        ht_done = sem("ht_done")
        hth_ready = sem("hth_ready")
        ht_ready = sem("ht_ready")
        dn_done = sem("dn_done")
        y_ready = sem("y_ready")
        y_stored = [sem(f"y_stored{n}") for n in range(4)]
        yg_in = [sem(f"yg_in{t}") for t in range(T - 1)]
        yg_last = [sem(f"yg_last{k}") for k in range(K)]
        shared_ready = sem("shared_ready")
        tail = sem("tail")
        var3_ready = sem("var3_ready")
        norm_ready = sem("norm_ready")
        rstd3_ready = sem("rstd3_ready")
        fin_ready = sem("fin_ready")
        out_stored = [sem(f"out_stored{n}") for n in range(2)]

        block = ctx.enter_context(nc.Block())

        JOBS = 5 + TB

        def released(n):
            b, j = divmod(n, JOBS)
            if j == 0:
                return qk_ready, 2 * b + 2
            if j in (1, 3):
                return gelu_ready, 6 * b + (j + 1) // 2
            return geglu_ready, 6 * b + (j // 2 if j < 5 else j - 2)

        def last_released(bank_no):
            return released(max(n for n in range(2 * JOBS) if 4 + n % 4 == bank_no))

        x_rows = x.rearrange("b (t p) d -> p (b t) d", p=P)
        out_rows = out.rearrange("b (t p) d -> p (b t) d", p=P)
        x1_rows = x1_dram.ap().rearrange("(t p) d -> t p d", p=P)
        y_rows = y_dram.ap()
        SLOT_RUN, SHARED_RUN = range(SLOTS), range(SLOTS, SLOTS + T)

        def among(tile, run):
            return not isinstance(tile, int) or tile in run

        def turn(t):
            b, i = divmod(t, TB)
            if b == B - 1:
                i = TB - 1 - i
            return b * TB + i, b, i

        LAG_PT, LAG_AV, LAG_PJ, LAG_FIN, LAG_XT, LAG_LG = 1, 2, 3, 4, 5, 6

        @block.sync
        def _(sp):
            sp.dma_start(x_sb[:, 0:TB, :], x_rows[:, 0:TB, :]).then_inc(ld_x[0], 16)
            sp.dma_start(cst[:, 0:P], consts[:, 0:P]).then_inc(ld_id, 16)
            sp.dma_start(sml[:, :], small).then_inc(ld_s, 16)
            sp.dma_start(ex_w[:, :, 0:X_VAL], expand[:, :, 0:X_VAL]).then_inc(ld_ex, 16)
            sp.dma_start(x_sb[:, TB:T, :], x_rows[:, TB:T, :]).then_inc(ld_x[1], 16)
            sp.dma_start(ex_w[:, :, X_VAL:NEXP], expand[:, :, X_VAL:NEXP]).then_inc(ld_val, 16)
            sp.dma_start(cst[:, P:NCONST], consts[:, P:NCONST]).then_inc(ld_c, 16)
            sp.dma_start(bias_e[:, :], rbias.to_broadcast([P, E])).then_inc(ld_b, 16)
            sp.dma_start(pj_w[:, :, :], project).then_inc(ld_pj, 16)
            sp.dma_start(rt_w[:, :, :], router).then_inc(ld_pj, 16)
            for e in range(RING):
                sp.dma_start(w_in[:, e, :], experts[:, e, :]).then_inc(ld_w[e], 16)
            with sp.Fori(1, EW // RING) as n:
                for j in range(RING):
                    sp.wait_ge(wlo_ready, RING * n + (j - RING + 1))
                    sp.dma_start(w_in[:, j, :], experts[:, bass.ds(RING * n + j, 1), :].rearrange("p o w -> p (o w)")).then_inc(ld_w[j], 16)

            for t in range(T):
                sp.wait_ge(x1_ready, t + 1)
                tile = turn(t)[0]
                sp.dma_start(x1_rows[tile], x1[:, tile, :]).then_inc(x1_stored, 16)

            with sp.Fori(0, SLOTS // 4) as n:
                for j in range(4):
                    sp.wait_ge(y_ready, 4 * n + (j + 1))
                    sp.dma_start(y_rows[bass.ds(n * (4 * P) + j * P, P), :], y_sb[:, j, :]).then_inc(y_stored[j], 16)
            for t in range(T):
                sp.wait_ge(fin_ready, t + 1)
                sp.dma_start(out_rows[:, t, :], fin[:, t % 2, :]).then_inc(out_stored[t % 2], 16)
            for n in range(2):
                sp.wait_ge(out_stored[n], 16 * T // 2)

        @block.gpsimd
        def _(pool):
            pool.wait_ge(consts_ready, 1)
            pool.wait_ge(ex_done, 2 * JOBS)
            pool.tensor_copy(ohr[:, :, :], iota16.unsqueeze(2).to_broadcast([P, P, T * K])).then_inc(counted, 1)
            pool.wait_ge(exp_ready, T)
            pool.tensor_copy(idt[:, :, :], iota16[:, 0:SLOTS].unsqueeze(2).to_broadcast([P, SLOTS, T * K])).then_inc(counted, 1)
            pool.wait_ge(x1_stored, 16 * T)
            pool.wait_ge(token_ready, 1)

            for m in range(SLOTS):
                if m >= AHEAD:
                    pool.wait_ge(xt_done, m - AHEAD + 1)
                pool.indirect_dma_start(
                    xg[:, m % AHEAD, :], None, x1_dram.ap(),
                    bass.IndirectOffsetOnAxis(ap=token[:, m:m + 1], axis=0)).then_inc(gath[m % AHEAD], 16)
            pool.wait_ge(slots_ready, 1)
            for j in range(4):
                pool.wait_ge(y_stored[j], 16 * SLOTS // 4)
            for t in range(T):
                for k in range(K):
                    n = t * K + k
                    pool.indirect_dma_start(
                        yg[:, n, :], None, y_rows,
                        bass.IndirectOffsetOnAxis(ap=slot_i[:, n:n + 1], axis=0)).then_inc(yg_in[t] if t < T - 1 else yg_last[k], 16)

        @block.tensor
        def _(pe):
            def turn_z(b):
                for c in range(DC):
                    for i in range(TB):
                        t = b * TB + i
                        pe.wait_ge(z_ready, t + 1)
                        mm = pe.transpose(bank[2 * b + c][:, i * P:(i + 1) * P],
                                          z_sb[:, t, c * P:(c + 1) * P], ident)
                    mm.then_inc(zt_done, 1)

            def expand_mm(n, rows, parts, lhs, rhs):
                if n >= 4:
                    pe.wait_ge(*released(n - 4))
                for c in range(DC):
                    mm = pe.matmul(bank[4 + n % 4][0:parts, 0:rows], lhs(c), rhs(c),
                                   start=(c == 0), stop=(c == DC - 1))
                mm.then_inc(ex_done, 1)

            pe.wait_ge(ld_id, 16)
            turn_z(0)
            for b in range(B):
                pe.wait_ge(h_ready, DC * (b + 1))
                pe.wait_ge(ld_ex, 16)
                toks = slice(b * S, (b + 1) * S)
                n = b * JOBS
                for j, (at, width) in enumerate([(X_Q, 2 * QK), (X_PRE, P), (X_LIN, P),
                                                 (X_PRE + P, P), (X_LIN + P, P)]):
                    expand_mm(n + j, S, width, lambda c: ex_w[:, c, at:at + width], lambda c: hT[:, c, toks])
                if b == 0:
                    turn_z(1)
                pe.wait_ge(ld_val, 16)
                for i in range(TB):
                    t = b * TB + i
                    expand_mm(n + 5 + i, 2 * D, P, lambda c: hT[:, c, t * P:(t + 1) * P],
                              lambda c: ex_w[:, c, X_VAL:X_VAL + 2 * D])

            def scores(t):
                tile, b, i = turn(t)
                pe.wait_ge(qk_ready, 2 * (b + 1))
                if t >= 2:
                    pe.wait_ge(smax_ready, t - 1)
                pe.matmul(bank[t % 2][:, 0:(i + 1) * P], qT[:, tile * P:(tile + 1) * P],
                          kT[:, b * S:b * S + (i + 1) * P], start=True, stop=True).then_inc(sc_done, 1)

            def turn_probs(t):
                pe.wait_ge(p_ready, t + 1)
                if t >= 1:
                    pe.wait_ge(pt_ready, t)
                for j in range(turn(t)[2] + 1):
                    mm = pe.transpose(bank[2][:, j * P:(j + 1) * P], p_sb[:, t % 2, j * P:(j + 1) * P], ident)
                mm.then_inc(pt_done, 1)

            def attend(t):
                tile, b, i = turn(t)
                pe.wait_ge(pt_ready, t + 1)
                pe.wait_ge(geglu_ready, 6 * b + 3 + i)
                if t == 0:
                    pe.wait_ge(*last_released(4))
                else:
                    pe.wait_ge(at_ready, t)
                for v in range(2):
                    for j in range(i + 1):
                        mm = pe.matmul(bank[4][:, v * P:(v + 1) * P], val[:, b * TB + j, v * P:(v + 1) * P],
                                       pT[:, j * P:(j + 1) * P], start=(j == 0), stop=(j == i))
                mm.then_inc(av_done, 1)

            def project_mm(t):
                tile, b, i = turn(t)
                pe.wait_ge(at_ready, t + 1)
                pe.wait_ge(ld_pj, 32)
                if t == 0:
                    pe.wait_ge(*last_released(5))
                else:
                    pe.wait_ge(y1_ready, t)
                for c in range(2 * DC):
                    lhs = locT[:, c, tile * P:(tile + 1) * P] if c < DC else aT[:, t % 2, (c - DC) * P:(c - DC + 1) * P]
                    mm = pe.matmul(bank[5][:, 0:D], lhs, pj_w[:, c, :], start=(c == 0), stop=(c == 2 * DC - 1))
                mm.then_inc(pj_done, 1)

            def turn_x1(t):
                pe.wait_ge(x1_ready, t + 1)
                if t == 0:
                    pe.wait_ge(*last_released(6))
                else:
                    pe.wait_ge(x1t_ready, t)
                for c in range(DC):
                    mm = pe.transpose(bank[6][:, c * P:(c + 1) * P], x1[:, turn(t)[0], c * P:(c + 1) * P], ident)
                mm.then_inc(x1t_done, 1)

            def logits(t):
                tile, b, i = turn(t)
                pe.wait_ge(x1t_ready, t + 1)
                if t == 0:
                    pe.wait_ge(*last_released(7))
                for c in range(DC):
                    mm = pe.matmul(bank[7 if b else 3][:, i * E:(i + 1) * E], x1T[:, c, tile * P:(tile + 1) * P],
                                   rt_w[:, c, :], start=(c == 0), stop=(c == DC - 1))
                mm.then_inc(lg_done, 1)

            for s in range(T + LAG_LG):
                for lag, stage in ((0, scores), (LAG_LG, logits), (LAG_XT, turn_x1), (LAG_PJ, project_mm),
                                   (LAG_AV, attend), (LAG_PT, turn_probs)):
                    if 0 <= s - lag < T:
                        stage(s - lag)

            XT, GU, HT, DN = (2, 7), (3, 4), (5, 6), (0, 1)

            def turn_rows(m, j, arrived):
                if isinstance(m, int) and m >= SLOTS:
                    rows = x1[:, m - SLOTS, :]
                else:
                    pe.wait_ge(gath[j % AHEAD], arrived)
                    rows = xg[:, j % AHEAD, :]
                for c in range(DC):
                    mm = pe.transpose(bank[XT[j % 2]][:, c * P:(c + 1) * P], rows[:, c * P:(c + 1) * P], ident)
                mm.then_inc(xt_done, 1)

            def three(dst, xs, ws):
                n = len(xs)
                for c in range(n):
                    for a_, b_ in ((0, 0), (0, 1), (1, 0)):
                        mm = pe.matmul(dst, xs[c][a_], ws[c][b_], start=(c == 0 and a_ + b_ == 0),
                                       stop=(c == n - 1 and a_ == 1))
                return mm

            def gate_up_mm(m, j, w):
                pe.wait_ge(xt_ready, m + 1)
                xs = [[xT[:, j % 4, (part * DC + c) * P:(part * DC + c + 1) * P] for part in range(2)] for c in range(DC)]
                three(bank[GU[j % 2]][:, 0:2 * I], xs, w[0:DC]).then_inc(gu_done, 1)

            def turn_h(m, j):
                pe.wait_ge(hh_ready, m + 1)
                pe.transpose(bank[HT[j % 2]][:, 0:P], hh[:, j % 2, :], ident).then_inc(ht_done, 1)

            def down_mm(m, j, w):
                if isinstance(m, int) and m in SLOT_RUN[-2:]:
                    pe.wait_ge(y_ready, m - 1)
                if isinstance(m, int) and m in SHARED_RUN[-2:]:
                    pe.wait_ge(shared_ready, m - 1 - SLOTS)
                pe.wait_ge(ht_ready, m + 1)
                three(bank[DN[j % 2]][:, 0:D], [[hTs[:, j % 4, part * P:(part + 1) * P] for part in range(2)]],
                      w[DC:DC + 1]).then_inc(dn_done, 1)

            def rank_mm(half):
                pe.wait_ge(oh_ready, half + 1)
                if half == 0:
                    pe.wait_ge(smax_ready, T - 1)
                for t in range(half * TB, (half + 1) * TB):
                    for k in range(K):
                        first = t == 0 and k == 0
                        n = T - t
                        rhs = oh[:, t, k, :].unsqueeze(1).to_broadcast([P, n, E])
                        pe.matmul(bank[0][:, (t + 1) * E:(T + 1) * E], ones16, rhs,
                                  start=first, stop=False, skip_group_check=True)
                        mm = pe.matmul(bank[0][:, t * E:(t + 1) * E], before16, oh[:, t, k, :],
                                       start=False, stop=(t == T - 1 and k == K - 1), skip_group_check=True)
                if half == 1:
                    mm.then_inc(pos_done, 1)

            def starts_mm():
                pe.wait_ge(ntcol_ready, 1)
                pe.wait_ge(smax_ready, T)
                pe.matmul(bank[1][:, 0:2 * E], ntcol[:, :].to_broadcast([E, P]), cst[0:E, C_TRI:C_TRI + 2 * E],
                          start=True, stop=True).then_inc(start_done, 1)

            def tile_experts_mm():
                pe.wait_ge(te_ready, 1)
                pe.matmul(bank[1][0:1, 0:P], te_col[:, :], ident, start=True, stop=True).then_inc(ter_done, 1)

            def token_list_mm():
                pe.wait_ge(ohr_ready, 1)
                for n in range(T * K):
                    if n % K == 0:
                        pe.wait_ge(idt_ready, n // K + 1)
                    mm = pe.matmul(bank[0][:, 0:SLOTS], ohr[:, :, n], idt[:, :, n],
                                   start=(n == 0), stop=(n == T * K - 1))
                mm.then_inc(list_done, 1)

            rank_mm(0)
            rank_mm(1)
            starts_mm()
            tile_experts_mm()
            token_list_mm()
            pe.wait_ge(te_loaded, 1)
            pe.wait_ge(wlo_ready, EW)
            pe.wait_ge(at_ready, T)
            pe.wait_ge(r_dve, 6)
            pe.wait_ge(token_ready, 1)

            def parts_at(e):
                return [[w[:, bass.ds(e + c * 2 * I, D)] for w in (w_hi, w_lo)] for c in range(DC + 1)]

            def weights_of(first, m, back, count):
                _, es = nc.values_load_multi_w_load_instructions(
                    te_row[0:1, bass.ds(m - back, back + count)], engines=[mybir.EngineType.PE],
                    min_val=0, max_val=(E - 1) * WE,
                    skip_runtime_bounds_check_because="the experts' numbers were bounded where they were counted")
                return {first - back + i: parts_at(e) for i, e in enumerate(es)}

            def step(m, j, run, weights, arrived):
                if among(m - 2, run):
                    turn_h(m - 2, j + 2)
                if among(m, run):
                    gate_up_mm(m, j, weights[j])
                if among(m + 2, run):
                    turn_rows(m + 2, j + 2, arrived[(j + 2) // AHEAD])
                if among(m - 4, run):
                    down_mm(m - 4, j, weights[j - 4])

            turn_rows(0, 0, 16)
            turn_rows(1, 1, 16)
            ws = weights_of(0, 0, 0, AHEAD)
            for m in range(AHEAD):
                step(m, m, SLOT_RUN, ws, [16, 32])
            with pe.Fori(1, SLOTS // AHEAD - 1) as n:
                ws = weights_of(0, AHEAD * n, 4, AHEAD)
                arrived = [pe.snap(16 * n + 16), pe.snap(16 * n + 32)]
                for j in range(AHEAD):
                    step(AHEAD * n + j, j, SLOT_RUN, ws, arrived)
            ws = weights_of(SLOTS - AHEAD, SLOTS - AHEAD, 4, AHEAD)
            for m in range(SLOTS - AHEAD, SLOTS + 4):
                step(m, m, SLOT_RUN, ws, {(m + 2) // AHEAD: 16 * SLOTS // AHEAD})
            turn_rows(SLOTS, SLOTS, None)
            turn_rows(SLOTS + 1, SLOTS + 1, None)
            ws = {m: parts_at(E * WE) for m in SHARED_RUN}
            for m in range(SLOTS, SLOTS + T + 4):
                step(m, m, SHARED_RUN, ws, {(m + 2) // AHEAD: None})

        @block.vector
        def _(dve):
            steps = [0]

            def mark(ins):
                steps[0] += 1
                ins.then_inc(vec, 1)
                return steps[0]

            def link(ins):
                dve.wait_ge(vec, mark(ins))

            def polish(cols):
                v, r, a, c = mv[:, cols, 1:2], rs[:, cols].unsqueeze(2), nt[:, cols, 0:1], nt[:, cols, 1:2]
                link(dve.scalar_tensor_tensor(out=a, in0=v, scalar=EPS, in1=r, op0=ALU.add, op1=ALU.mult))
                link(dve.scalar_tensor_tensor(out=c, in0=a, scalar=-0.5, in1=r, op0=ALU.mult, op1=ALU.mult))
                link(dve.scalar_tensor_tensor(out=r, in0=c, scalar=1.5, in1=r, op0=ALU.add, op1=ALU.mult))

            def split_lo(e):
                dve.wait_ge(whi_ready, e + 1)
                cols = slice(e * WE, (e + 1) * WE)
                dve.scalar_tensor_tensor(out=w_lo[:, cols], in0=w_in[:, e % RING, :], scalar=UP, in1=w_hi[:, cols],
                                         op0=ALU.mult, op1=ALU.subtract).then_inc(wlo_ready, 1)

            for b in range(B):
                dve.wait_ge(ld_x[b], 16)
                for t in range(b * TB, (b + 1) * TB):
                    ins = dve.bn_stats(bst[:, t, :], x_sb[:, t, :])
                link(ins)
                for t in range(b * TB, (b + 1) * TB):
                    ins = dve.bn_aggr(mv[:, t, :], bst[:, t, :])
                ins.then_inc(var_ready, 1)
                dve.wait_ge(rstd_ready, b + 1)
                dve.wait_ge(var_ready, b + 1)
                polish(slice(b * TB, (b + 1) * TB))
                for t in range(b * TB, (b + 1) * TB):
                    dve.tensor_scalar(z_sb[:, t, :], x_sb[:, t, :], mv[:, t, 0:1], rs[:, t:t + 1],
                                      ALU.subtract, ALU.mult).then_inc(z_ready, 1)
            dve.wait_ge(ld_id, 16)
            dve.wait_ge(ld_c, 16)
            dve.tensor_copy(sc16[:, :], cst[:, 0:4 * P]).then_inc(consts_ready, 1)
            dve.wait_ge(pos_ready, 1)
            link(dve.scalar_tensor_tensor(out=pb[:, 3:4], in0=sml[:, 2 * DC:2 * DC + 1], scalar=0.0,
                                          in1=pb[:, 2:3], op0=ALU.max, op1=ALU.add))
            link(dve.scalar_tensor_tensor(out=bmat[:, :], in0=cst[:, C_REL:C_REL + S], scalar=pb[:, 3:4],
                                          in1=cst[:, C_MASK:C_MASK + S], op0=ALU.mult, op1=ALU.add))
            experts_left = iter(range(EW))
            for b in range(B):
                for _ in range(2):
                    split_lo(next(experts_left))
                for c in range(2):
                    dve.wait_ge(ex_done, b * JOBS + 3 + 2 * c)
                    dve.wait_ge(gelu_ready, 6 * b + c + 1)
                    dve.tensor_tensor(locT[:, c, b * S:(b + 1) * S], bank[4 + (b * JOBS + 2 + 2 * c) % 4][:, :],
                                      gl[:, c, :], ALU.mult).then_inc(geglu_ready, 1)
                    split_lo(next(experts_left))
                for i in range(TB):
                    dve.wait_ge(gelu_ready, 6 * b + 3 + i)
                    dve.tensor_tensor(val[:, b * TB + i, :], bank[4 + (b * JOBS + 5 + i) % 4][:, 0:D],
                                      gv[:, i % 2, :], ALU.mult).then_inc(geglu_ready, 1)
                    split_lo(next(experts_left))

            def attention_step(s):
                fin, res, nrm = (s - lag if 0 <= s - lag < T else None for lag in (LAG_FIN, LAG_PJ, LAG_PT))
                if fin is not None:
                    tile = turn(fin)[0]
                    v, r, a, c = mv[:, tile, 1:2], rs[:, tile:tile + 1], nt[:, tile, 0:1], nt[:, tile, 1:2]
                    dve.wait_ge(rstd2_ready, fin + 1)
                    polished = mark(dve.scalar_tensor_tensor(out=a, in0=v, scalar=EPS, in1=r, op0=ALU.add, op1=ALU.mult))
                if nrm is not None:
                    n_tile, b, i = turn(nrm)
                    probs = p_sb[:, nrm % 2, 0:(i + 1) * P]
                    dve.wait_ge(exp_ready, nrm + 1)
                    inverted = mark(dve.reciprocal(mxs[:, n_tile, 2:3], mxs[:, n_tile, 1:2]))
                if fin is not None:
                    dve.wait_ge(vec, polished)
                    polished = mark(dve.scalar_tensor_tensor(out=c, in0=a, scalar=-0.5, in1=r, op0=ALU.mult, op1=ALU.mult))
                if nrm is not None:
                    dve.wait_ge(vec, inverted)
                    dve.tensor_scalar(probs, probs, mxs[:, n_tile, 2:3], None, ALU.mult).then_inc(p_ready, 1)
                if fin is not None:
                    dve.wait_ge(vec, polished)
                    link(dve.scalar_tensor_tensor(out=r, in0=c, scalar=1.5, in1=r, op0=ALU.add, op1=ALU.mult))
                    dve.wait_ge(zt_done, B * DC)
                    dve.tensor_scalar(x1[:, tile, :], y1[:, fin % 2, :], mv[:, tile, 0:1], rs[:, tile:tile + 1],
                                      ALU.subtract, ALU.mult).then_inc(x1_ready, 1)
                if res is not None:
                    r_tile, rows = turn(res)[0], y1[:, res % 2, :]
                    dve.wait_ge(pj_done, res + 1)
                    if res >= 2:
                        dve.wait_ge(x1_ready, res - 1)
                    link(dve.scalar_tensor_tensor(out=rows, in0=x_sb[:, r_tile, :], scalar=2.0,
                                                  in1=bank[5][:, 0:D], op0=ALU.mult, op1=ALU.add))
                    taken = mark(dve.bn_stats(bst[:, r_tile, :], rows))
                if s < T:
                    m_tile, b, i = turn(s)
                    w = (i + 1) * P
                    dve.wait_ge(sc_done, s + 1)
                    if s >= 2:
                        dve.wait_ge(exp_ready, s - 1)
                    dve.tensor_tensor_reduce(s_sb[:, s % 2, 0:w], bank[s % 2][:, 0:w], bmat[:, S - w:S], 1.0,
                                             3.0 * FAR, ALU.add, ALU.min, mxs[:, m_tile, 0:1]).then_inc(smax_ready, 1)
                if res is not None:
                    dve.wait_ge(vec, taken)
                    dve.bn_aggr(mv[:, r_tile, :], bst[:, r_tile, :]).then_inc(y1_ready, 1)

            def half(h):
                ts = slice(h * TB, (h + 1) * TB)
                return [b[:, ts, :] for b in (lg, ra, re_, rb, rc, score, sel)]

            def logits_out(h):
                l = half(h)[0]
                dve.wait_ge(lg_done, (h + 1) * TB)
                dve.tensor_copy(l, bank[7 if h else 3][:, 0:TB * E].rearrange("p (t e) -> p t e", e=E)).then_inc(r_dve, 1)

            def one_plus(h):
                l, a, e, u, d, q, c = half(h)
                dve.wait_ge(r_act, 3 * h + 1)
                dve.tensor_scalar(u, e, 1.0, None, ALU.add).then_inc(r_dve, 1)
                dve.wait_ge(r_dve, 3 * h + 2)
                link(dve.scalar_tensor_tensor(out=d, in0=u, scalar=-1.0, in1=e, op0=ALU.add, op1=ALU.subtract))

            def softplus(h):
                l, a, e, u, d, q, c = half(h)
                dve.wait_ge(r_act, 3 * h + 2)
                link(dve.scalar_tensor_tensor(out=a, in0=l, scalar=0.0, in1=a, op0=ALU.max, op1=ALU.add))
                link(dve.tensor_tensor(a, a, d, ALU.subtract))
                dve.tensor_scalar(a, a, 2.0 ** -110, None, ALU.max).then_inc(r_dve, 1)

            def root(h):
                l, a, e, u, d, q, c = half(h)
                dve.wait_ge(r_dve, 3 * h + 3)
                dve.wait_ge(r_act, 3 * h + 3)
                link(dve.tensor_tensor(e, a, u, ALU.mult))
                link(dve.scalar_tensor_tensor(out=d, in0=e, scalar=-0.5, in1=u, op0=ALU.mult, op1=ALU.mult))
                link(dve.scalar_tensor_tensor(out=q, in0=d, scalar=1.5, in1=e, op0=ALU.add, op1=ALU.mult))

            def greatest(h):
                l, a, e, u, d, q, c = half(h)
                link(dve.tensor_tensor(c, q, bias_e[:, :].unsqueeze(1).to_broadcast([P, TB, E]), ALU.add))
                for t in range(h * TB, (h + 1) * TB):
                    ins = dve.max(top[:, t, :], sel[:, t, :])
                link(ins)

            def one_hots(h):
                ts = slice(h * TB, (h + 1) * TB)
                for t in range(h * TB, (h + 1) * TB):
                    ins = dve.max_index(topi[:, t, :], top[:, t, :], sel[:, t, :])
                link(ins)
                link(dve.tensor_copy(topf[:, ts, :], topi[:, ts, 0:K]))
                dve.tensor_tensor(oh[:, ts, :, :],
                                  iota16[:, 0:E].unsqueeze(1).unsqueeze(1).to_broadcast([P, TB, K, E]),
                                  topf[:, ts, :].unsqueeze(3).to_broadcast([P, TB, K, E]),
                                  ALU.is_equal).then_inc(oh_ready, 1)

            def chosen_scores(h):
                ts = slice(h * TB, (h + 1) * TB)
                dve.wait_ge(oh_ready, h + 1)
                link(dve.tensor_tensor(prod[:, ts, :, :], oh[:, ts, :, :],
                                       score[:, ts, :].unsqueeze(2).to_broadcast([P, TB, K, E]), ALU.mult))
                link(dve.tensor_reduce(pk[:, ts, :], prod[:, ts, :, :], AX, ALU.add))

            def shares():
                link(dve.tensor_reduce(psum_k[:, :, 0:1], pk[:, :, :], AX, ALU.add))
                link(dve.tensor_scalar(psum_k[:, :, 0:1], psum_k[:, :, 0:1], 1e-20, None, ALU.add))
                link(dve.reciprocal(psum_k[:, :, 1:2], psum_k[:, :, 0:1]))
                link(dve.tensor_tensor(pk[:, :, :], pk[:, :, :], psum_k[:, :, 1:2].to_broadcast([P, T, K]), ALU.mult))

            def count_tiles():
                dve.wait_ge(pos_done, 1)
                link(dve.tensor_scalar(ntile_i[:, :], bank[0][:, T * E:(T + 1) * E], float(P - 1), None, ALU.add))
                link(dve.tensor_scalar(ntile_j[:, :], ntile_i[:, :], 7, None, ALU.logical_shift_right))
                link(dve.tensor_copy(ntile[:, :], ntile_j[:, :]))
                dve.tensor_tensor_reduce(ntd[:, :], ntile[0:E, :], ident[0:E, 0:E], 1.0, 0.0, ALU.mult, ALU.add,
                                         ntcol[:, :]).then_inc(ntcol_ready, 1)

            def tile_experts():
                dve.wait_ge(start_done, 1)
                dve.tensor_scalar(base[:, :], bank[1][:, 0:E], float(P), None, ALU.mult)
                link(dve.tensor_copy(ends[:, :], bank[1][:, E:2 * E]))
                link(dve.tensor_scalar(ends[:, :], ends[:, :], cst[:, C_PID:C_PID + 1], None, ALU.is_le, ALU.add,
                                       accum_out=te_col[:, :]))
                dve.tensor_scalar(te_col[:, :], te_col[:, :], float(E - 1), None, ALU.min).then_inc(te_ready, 1)

            def find_slots():
                link(dve.tensor_tensor(posb[:, :, :], bank[0][:, 0:T * E].rearrange("p (t e) -> p t e", e=E),
                                       base[:, :].unsqueeze(1).to_broadcast([P, T, E]), ALU.add))
                link(dve.tensor_tensor(prod[:, :, :, :], oh[:, :, :, :],
                                       posb[:, :, :].unsqueeze(2).to_broadcast([P, T, K, E]), ALU.mult))
                link(dve.tensor_reduce(slot_f[:, :].rearrange("p (t k) -> p t k", k=K), prod[:, :, :, :], AX, ALU.add))
                link(dve.tensor_copy(slot_i[:, :], slot_f[:, :]))
                dve.tensor_scalar(slot_t[:, 0, :], slot_i[:, :], 7, None, ALU.logical_shift_right)
                link(dve.tensor_scalar(slot_t[:, 1, :], slot_i[:, :], P - 1, None, ALU.bitwise_and))
                dve.tensor_copy(slot_r[:, :, :], slot_t[:, :, :]).then_inc(slotr_ready, 1)
                dve.wait_ge(slotr_ready, 1)

            def expert_rows():
                dve.wait_ge(ter_done, 1)
                dve.tensor_scalar(te_row[:, :], bank[1][0:1, 0:SLOTS], float(WE), None, ALU.mult).then_inc(te_loaded, 1)

            def list_operands():
                dve.wait_ge(counted, 2)
                dve.tensor_tensor(idt[:, :, :], idt[:, :, :],
                                  slot_r[:, 0, :].unsqueeze(1).to_broadcast([P, SLOTS, T * K]), ALU.is_equal).then_inc(tile1h_ready, 1)
                dve.tensor_tensor(ohr[:, :, :], ohr[:, :, :],
                                  slot_r[:, 1, :].unsqueeze(1).to_broadcast([P, P, T * K]), ALU.is_equal).then_inc(ohr_ready, 1)

            def token_list():
                dve.wait_ge(list_done, 1)
                dve.tensor_copy(token[:, :], bank[0][:, 0:SLOTS]).then_inc(token_ready, 1)

            def low_xT(m, j):
                dve.wait_ge(xth_ready, m + 1)
                dve.tensor_tensor(xT[:, j % 4, D:2 * D], bank[(2, 7)[j % 2]][:, 0:D], xT[:, j % 4, 0:D],
                                  ALU.subtract).then_inc(xt_ready, 1)

            def clip(m, j):
                dve.wait_ge(gu_done, m + 1)
                dve.tensor_scalar(gu[:, j % 2, :], bank[(3, 4)[j % 2]][:, 0:2 * I], ALPHA * UP, -ALPHA * UP,
                                  ALU.min, ALU.max).then_inc(clipped, 1)

            def low_hT(m, j):
                dve.wait_ge(hth_ready, m + 1)
                dve.tensor_tensor(hTs[:, j % 4, P:2 * P], bank[(5, 6)[j % 2]][:, 0:P], hTs[:, j % 4, 0:P],
                                  ALU.subtract).then_inc(ht_ready, 1)

            def gate_times_up(m, j):
                dve.wait_ge(silu_ready, m + 1)
                dve.tensor_tensor(hh[:, j % 2, :], sg[:, j % 2, :], gu[:, j % 2, I:2 * I], ALU.mult).then_inc(hh_ready, 1)

            for s in range(T + LAG_LG):
                attention_step(s)
                if s == TB + LAG_LG:
                    one_plus(0)
                for e in islice(experts_left, min(s, 2)):
                    split_lo(e)
                if s == TB + LAG_LG - 1:
                    logits_out(0)
                if s == TB + LAG_LG:
                    softplus(0)
                if s == TB + LAG_LG + 1:
                    root(0)
            dve.wait_ge(consts_ready, 1)
            dve.wait_ge(ld_b, 16)
            greatest(0)
            logits_out(1)
            one_hots(0)
            one_plus(1)
            softplus(1)
            root(1)
            greatest(1)
            one_hots(1)
            chosen_scores(1)

            count_tiles()
            tile_experts()
            find_slots()
            expert_rows()
            list_operands()
            token_list()
            chosen_scores(0)
            shares()
            dve.drain().then_inc(slots_ready, 1)

            def shared_rows(m):
                dve.wait_ge(dn_done, m + 1)
                dve.scalar_tensor_tensor(out=shared[:, m - SLOTS, :], in0=bank[m % 2][:, 0:D], scalar=1.0 / (UP * UP),
                                         in1=x1[:, m - SLOTS, :], op0=ALU.mult, op1=ALU.add).then_inc(shared_ready, 1)

            def step(m, j, run):
                if run == SHARED_RUN and among(m - 5, run):
                    shared_rows(m - 5)
                if among(m - 1, run):
                    gate_times_up(m - 1, j + 3)
                if among(m - 2, run):
                    low_hT(m - 2, j + 2)
                if among(m, run):
                    clip(m, j)
                if among(m + 2, run):
                    low_xT(m + 2, j + 2)

            low_xT(0, 0)
            low_xT(1, 1)
            for m in range(4):
                step(m, m, SLOT_RUN)
            with dve.Fori(1, SLOTS // 4 - 1) as n:
                for j in range(4):
                    step(4 * n + j, j, SLOT_RUN)
            for m in range(SLOTS - 4, SLOTS + 2):
                step(m, m, SLOT_RUN)
            low_xT(SLOTS, SLOTS)
            low_xT(SLOTS + 1, SLOTS + 1)
            for m in range(SLOTS, SLOTS + T + 5):
                step(m, m, SHARED_RUN)
            dve.wait_ge(shared_ready, T)

            done = [0]

            def mark(ins):
                ins.then_inc(tail, 1)
                done[0] += 1
                return done[0]

            def add_expert(t, k, before):
                a = acc[:, t % 2, :]
                if t == T - 1:
                    dve.wait_ge(yg_last[k], 16)
                elif k == 0:
                    dve.wait_ge(yg_in[t], 16 * K)
                if k == 0 and t >= 2:
                    dve.wait_ge(fin_ready, t - 1)
                if k > 0:
                    dve.wait_ge(tail, before)
                return mark(dve.scalar_tensor_tensor(
                    out=a, in0=yg[:, t * K + k, :], scalar=pk[:, t, k:k + 1],
                    in1=shared[:, t, :] if k == 0 else a, op0=ALU.mult, op1=ALU.add))

            def polish_part(t, i, before):
                v, r, a, c = mv[:, t, 1:2], rs[:, t:t + 1], nt[:, t, 0:1], nt[:, t, 1:2]
                if i == 0:
                    dve.wait_ge(rstd3_ready, t + 1)
                    return mark(dve.scalar_tensor_tensor(out=a, in0=v, scalar=EPS, in1=r, op0=ALU.add, op1=ALU.mult))
                dve.wait_ge(tail, before)
                if i == 1:
                    return mark(dve.scalar_tensor_tensor(out=c, in0=a, scalar=-0.5, in1=r, op0=ALU.mult, op1=ALU.mult))
                if i == 2:
                    return mark(dve.scalar_tensor_tensor(out=r, in0=c, scalar=1.5, in1=r, op0=ALU.add, op1=ALU.mult))
                dve.scalar_tensor_tensor(out=a, in0=mv[:, t, 0:1], scalar=-1.0, in1=r,
                                         op0=ALU.mult, op1=ALU.mult).then_inc(norm_ready, 1)

            added = polished = None
            for t in range(T + 1):
                for i in range(K):
                    if t < T:
                        added = add_expert(t, i, added)
                    if t >= 1:
                        polished = polish_part(t - 1, i, polished)
                if t < T:
                    dve.wait_ge(tail, added)
                    dve.wait_ge(tail, mark(dve.bn_stats(bst[:, t, :], acc[:, t % 2, :])))
                    dve.bn_aggr(mv[:, t, :], bst[:, t, :]).then_inc(var3_ready, 1)

        @block.scalar
        def _(act):
            steps = [0]

            def link(ins):
                steps[0] += 1
                ins.then_inc(act_, 1)
                act.wait_ge(act_, steps[0])

            def rstd(cols, ready):
                r = rs[:, cols].unsqueeze(2)
                act.activation(r, mv[:, cols, 1:2], ACT.Ln, bias=EPS).then_inc(act_, 1)
                steps[0] += 1
                act.wait_ge(act_, steps[0])
                act.activation(r, r, ACT.Exp, scale=-0.5).then_inc(ready, 1)

            def load_ln_exp():
                act.add_instruction(mybir.InstLoadActFuncSet(
                    act_func_set_id=LN_EXP_SET, name=nc.get_next_instruction_name(), engine=mybir.EngineType.Activation))

            def split_hi(e):
                act.wait_ge(ld_w[e % RING], 16 * (e // RING + 1))
                act.activation(w_hi[:, e * WE:(e + 1) * WE], w_in[:, e % RING, :], ACT.Copy, scale=UP).then_inc(whi_ready, 1)

            def copy_hT(b):
                for c in range(DC):
                    act.wait_ge(zt_done, b * DC + c + 1)
                    act.activation(hT[:, c, b * S:(b + 1) * S], bank[2 * b + c][:, :], ACT.Identity,
                                   bias=sml[:, DC + c:DC + c + 1], scale=sml[:, c:c + 1]).then_inc(h_ready, 1)

            load_ln_exp()
            act.wait_ge(var_ready, 1)
            rstd(slice(0, TB), rstd_ready)
            act.wait_ge(ld_s, 16)
            link(act.activation(pb[:, 0:1], sml[:, 2 * DC:2 * DC + 1], ACT.Abs))
            link(act.activation(pb[:, 1:2], pb[:, 0:1], ACT.Exp, scale=-1.0))
            act.activation(pb[:, 2:3], pb[:, 1:2], ACT.Ln, bias=1.0).then_inc(pos_ready, 1)
            copy_hT(0)
            act.wait_ge(var_ready, 2)
            rstd(slice(TB, T), rstd_ready)
            experts_left = iter(range(EW))
            for b in range(B):
                n = b * JOBS
                cols = slice(b * S, (b + 1) * S)
                act.wait_ge(ex_done, n + 1)
                act.activation(qT[:, cols], bank[4 + n % 4][0:QK, :], ACT.Copy, scale=-float(QK) ** -0.5).then_inc(qk_ready, 1)
                act.activation(kT[:, cols], bank[4 + n % 4][QK:2 * QK, :], ACT.Copy).then_inc(qk_ready, 1)
                split_hi(next(experts_left))
                split_hi(next(experts_left))
                for c in range(2):
                    act.wait_ge(ex_done, n + 2 + 2 * c)
                    if b:
                        act.wait_ge(geglu_ready, 6 * (b - 1) + c + 1)
                    act.activation(gl[:, c, :], bank[4 + (n + 1 + 2 * c) % 4][:, :], ACT.Gelu).then_inc(gelu_ready, 1)
                    split_hi(next(experts_left))
                if b == 0:
                    copy_hT(1)
                for i in range(TB):
                    act.wait_ge(ex_done, n + 6 + i)
                    if i >= 2:
                        act.wait_ge(geglu_ready, 6 * b + 3 + i - 2)
                    elif b:
                        act.wait_ge(geglu_ready, 6 * (b - 1) + 3 + TB - 2 + i)
                    act.activation(gv[:, i % 2, :], bank[4 + (n + 5 + i) % 4][:, D:2 * D], ACT.Gelu).then_inc(gelu_ready, 1)
                    split_hi(next(experts_left))

            load_ln_exp()

            def exps(t):
                tile, b, i = turn(t)
                w = (i + 1) * P
                act.wait_ge(smax_ready, t + 1)
                if t >= 2:
                    act.wait_ge(pt_done, t - 1)
                act.activation(p_sb[:, t % 2, 0:w], s_sb[:, t % 2, 0:w], ACT.Exp, bias=mxs[:, tile, 0:1], scale=-1.0,
                               accum_out=mxs[:, tile, 1:2]).then_inc(exp_ready, 1)

            def copy_pT(t):
                tile, b, i = turn(t)
                w = (i + 1) * P
                act.wait_ge(pt_done, t + 1)
                if t >= 1:
                    act.wait_ge(av_done, t)
                act.activation(pT[:, 0:w], bank[2][:, 0:w], ACT.Copy).then_inc(pt_ready, 1)

            def copy_aT(t):
                act.wait_ge(av_done, t + 1)
                if t >= 2:
                    act.wait_ge(pj_done, t - 1)
                act.activation(aT[:, t % 2, :], bank[4][:, 0:D], ACT.Copy).then_inc(at_ready, 1)

            def rstd2(t):
                act.wait_ge(y1_ready, t + 1)
                tile = turn(t)[0]
                rstd(slice(tile, tile + 1), rstd2_ready)

            def copy_x1T(t):
                tile = turn(t)[0]
                act.wait_ge(x1t_done, t + 1)
                act.wait_ge(ex_done, 2 * JOBS)
                act.activation(x1T[:, :, tile * P:(tile + 1) * P], bank[6][:, 0:D].rearrange("p (c n) -> p c n", c=DC),
                               ACT.Copy).then_inc(x1t_ready, 1)

            def exp_of_logits(h):
                ts = slice(h * TB, (h + 1) * TB)
                act.wait_ge(r_dve, 3 * h + 1)
                link(act.activation(ra[:, ts, :], lg[:, ts, :], ACT.Abs))
                act.activation(re_[:, ts, :], ra[:, ts, :], ACT.Exp, scale=-1.0).then_inc(r_act, 1)

            def ln_of_sum(h):
                ts = slice(h * TB, (h + 1) * TB)
                act.wait_ge(r_dve, 3 * h + 2)
                act.activation(ra[:, ts, :], rb[:, ts, :], ACT.Ln).then_inc(r_act, 1)

            def inverse_root(h):
                ts = slice(h * TB, (h + 1) * TB)
                act.wait_ge(r_dve, 3 * h + 3)
                link(act.activation(rb[:, ts, :], ra[:, ts, :], ACT.Ln, scale=2.0 ** SQ_UP))
                act.activation(rb[:, ts, :], rb[:, ts, :], ACT.Exp, scale=-0.5, bias=0.5 * SQ_UP * LN2).then_inc(r_act, 1)

            for s in range(T + LAG_LG):
                for lag, stage in ((LAG_XT, copy_x1T), (None, split_hi), (LAG_AV, copy_aT), (LAG_PJ, rstd2),
                                   (LAG_PT, copy_pT), (0, exps), (None, split_hi)):
                    if lag is None:
                        for e in islice(experts_left, int(s >= 1)):
                            stage(e)
                    elif 0 <= s - lag < T:
                        stage(s - lag)
                if s == TB + LAG_LG - 1:
                    exp_of_logits(0)
                if s == TB + LAG_LG:
                    ln_of_sum(0)
                if s == TB + LAG_LG + 1:
                    inverse_root(0)
            exp_of_logits(1)
            ln_of_sum(1)
            inverse_root(1)

            act.wait_ge(tile1h_ready, 1)
            for t in range(T):
                part = idt[:, :, t * K:(t + 1) * K]
                act.activation(part, part, ACT.Copy, scale=cst[:, C_TOK + t:C_TOK + t + 1]).then_inc(idt_ready, 1)

            def high_xT(m, j):
                act.wait_ge(xt_done, m + 1)
                act.activation(xT[:, j % 4, 0:D], bank[(2, 7)[j % 2]][:, 0:D], ACT.Copy).then_inc(xth_ready, 1)

            def silu(m, j):
                act.wait_ge(clipped, m + 1)
                act.activation(sg[:, j % 2, :], gu[:, j % 2, 0:I], ACT.Silu, scale=1.0 / UP).then_inc(silu_ready, 1)

            def high_hT(m, j):
                act.wait_ge(ht_done, m + 1)
                act.activation(hTs[:, j % 4, 0:P], bank[(5, 6)[j % 2]][:, 0:P], ACT.Copy).then_inc(hth_ready, 1)

            def copy_y(m, j):
                if not (isinstance(m, int) and m < 4):
                    act.wait_ge(y_stored[j % 4], 16 * (m // 4) if isinstance(m, int) else 4 * m - 4 * (j % 4))
                act.wait_ge(dn_done, m + 1)
                act.activation(y_sb[:, j % 4, :], bank[j % 2][:, 0:D], ACT.Copy, scale=1.0 / (UP * UP)).then_inc(y_ready, 1)

            def step(m, j, run):
                if run == SLOT_RUN and among(m - 5, run):
                    copy_y(m - 5, j + 3)
                if among(m - 1, run):
                    silu(m - 1, j + 3)
                if among(m - 2, run):
                    high_hT(m - 2, j + 2)
                if among(m + 2, run):
                    high_xT(m + 2, j + 2)

            high_xT(0, 0)
            high_xT(1, 1)
            for m in range(12):
                step(m, m, SLOT_RUN)
            with act.Fori(3, SLOTS // 4 - 1) as n:
                for j in range(4):
                    step(4 * n + j, j, SLOT_RUN)
            for m in range(SLOTS - 4, SLOTS + 5):
                step(m, m, SLOT_RUN)
            high_xT(SLOTS, SLOTS)
            high_xT(SLOTS + 1, SLOTS + 1)
            for m in range(SLOTS, SLOTS + T + 2):
                step(m, m, SHARED_RUN)
            load_ln_exp()

            def finish(t):
                act.wait_ge(norm_ready, t + 1)
                if t >= 2:
                    act.wait_ge(out_stored[t % 2], 16 * (t // 2))
                act.activation(fin[:, t % 2, :], acc[:, t % 2, :], ACT.Identity,
                               bias=nt[:, t, 0:1], scale=rs[:, t:t + 1]).then_inc(fin_ready, 1)

            for t in range(T + 1):
                if t >= 1:
                    finish(t - 1)
                if t < T:
                    act.wait_ge(var3_ready, t + 1)
                    rstd(slice(t, t + 1), rstd3_ready)


def _constants(np):
    c = np.zeros((P, NCONST), np.float32)
    p = np.arange(P)[:, None]
    n = np.arange(P)[None, :]
    c[:, C_ID:C_ID + P] = p == n
    c[:, C_LT:C_LT + P] = p < n
    c[:, C_ONE:C_ONE + P] = 1.0
    c[:, C_IOTA:C_IOTA + P] = n
    rel = np.arange(S)[None, :] - (S - P) - p
    c[:, C_REL:C_REL + S] = np.maximum(-rel, 0)
    c[:, C_MASK:C_MASK + S] = np.where(rel > 0, FAR, 0.0)
    c[:, C_TOK:C_TOK + T] = np.arange(T)[None, :] * P + p
    c[:, C_PID:C_PID + 1] = p
    e = np.arange(E)[None, :]
    c[:, C_TRI:C_TRI + E] = p < e
    c[:, C_TRI + E:C_TRI + 2 * E] = p <= e
    return c


def kernel(**inputs):
    import numpy as np
    import concourse.bacc as bacc
    from concourse.bass_utils import run_bass_kernel_spmd as run

    a = {k: np.asarray(v) for k, v in inputs.items()}

    def chunked(w, lead):
        return w.T.reshape(lead, P, w.shape[0]).transpose(1, 0, 2)

    ex = a["L0_attn_expand"]
    loc, value = 2 * QK, 2 * QK + LOC
    pre = 2 * QK + 2 * D
    ex = np.concatenate([ex[0:2 * QK], ex[loc:loc + D], ex[pre:pre + D], ex[value:value + D], ex[pre + D:pre + 2 * D]])
    gate = np.concatenate([a["L0_ffn_gate_w"], a["L0_ffn_shared_gate_w"][None]])
    up = np.concatenate([a["L0_ffn_up_w"], a["L0_ffn_shared_up_w"][None]])
    dn = np.concatenate([a["L0_ffn_down_w"], a["L0_ffn_shared_down_w"][None]])
    gu = np.concatenate([gate, up], axis=1)
    gu = gu.transpose(2, 0, 1).reshape(DC, P, EW, 2 * I).transpose(1, 2, 0, 3).reshape(P, EW, 2 * 2 * I)
    small = np.concatenate([a["L0_attn_ln_gamma"].reshape(DC, P).T, a["L0_attn_ln_beta"].reshape(DC, P).T,
                            np.broadcast_to(a["L0_attn_pos_mult"].reshape(1, 1), (P, 1))], axis=1)
    arrays = {
        "x": a["L0_attn_x"],
        "consts": _constants(np),
        "small": small,
        "rbias": a["L0_ffn_expert_bias"].reshape(1, E),
        "expand": chunked(ex, DC),
        "project": chunked(a["L0_attn_project"], 2 * DC),
        "router": chunked(a["L0_ffn_router_w"], DC),
        "experts": np.concatenate([gu, dn.transpose(2, 0, 1)], axis=2),
    }
    arrays = {k: np.ascontiguousarray(v) for k, v in arrays.items()}
    nc = bacc.Bacc("TRN2", target_bir_lowering=False, num_devices=1)
    args = {k: nc.dram_tensor(f"in_{k}", v.shape, mybir.dt.from_np(v.dtype), kind="ExternalInput").ap()
            for k, v in arrays.items()}
    args["out"] = nc.dram_tensor("out_0", (B, S, D), F32, kind="ExternalOutput").ap()
    attn_moe_program(nc, **args)
    r = run(nc, [{f"in_{k}": v for k, v in arrays.items()}], core_ids=[0])
    return r.results[0]["out_0"]
```
